# Optimizing a Trainium2 kernel written in Bass

```python
import numpy as np
import jax
import jax.numpy as jnp

def _softmax(x, axis=-1):
    return jax.nn.softmax(x, axis=axis)

def _gelu(x):
    return jax.nn.gelu(x, approximate=True)

def _silu(x):
    return jax.nn.silu(x)

def _sigmoid(x):
    return jax.nn.sigmoid(x)

def _layernorm(x, axis=-1, eps=1e-05):
    m = jnp.mean(x, axis=axis, keepdims=True)
    v = jnp.var(x, axis=axis, keepdims=True)
    return (x - m) / jnp.sqrt(v + eps)

def _scatter_add(tgt, idx, src, axis=0):
    return tgt.at[idx].add(src)

def _segment_sum(src, seg, n):
    return jax.ops.segment_sum(src, seg, n)
kernel_name = 'mk_cond_resid_d2_seqx_r4_f08289'

def setup_inputs(seed: int=0):
    np.random.seed(seed)
    _w = jnp.asarray

    def _rec_inputs():
        import jax
        import jax.numpy as jnp
        _rk = jax.random.key(seed)
        x = -0.0002928 + 1 * jax.random.normal(jax.random.fold_in(_rk, 1), (8, 512, 256), jnp.float32)
        _lenS = 512 - jax.random.randint(jax.random.fold_in(_rk, 7), (8,), 0, max(1, 512 // 4) + 1, jnp.int32)
        _lenS2 = 512 - jax.random.randint(jax.random.fold_in(_rk, 8), (8,), 0, max(1, 512 // 4) + 1, jnp.int32)
        cond_1024 = 0.0061147 + 1.02565 * jax.random.normal(jax.random.fold_in(_rk, 11), (8, 256), jnp.float32)
        return (x, cond_1024)
    x, cond_1024 = _rec_inputs()

    def _L0_cond_setup():
        import jax, jax.numpy as jnp
        import numpy as np
        D, HS, HE, E, K = (256, 512, 256, 8, 2)
        B, T = (4, 256)
        N_SHARED = 1
        key = jax.random.key(seed)
        ks = jax.random.split(key, 9)
        g = lambda k, shape, s: jax.random.normal(k, shape, jnp.float32) * s
        return {'x': g(ks[0], (B, T, D), 1.0), 't_emb': g(ks[1], (B, D), 1.0), 'router_W': g(ks[2], (2 * D, E), 0.01), 'router_bias': jnp.zeros((E,), jnp.float32), 'w1': g(ks[3], (D, HS), 0.02), 'w3': g(ks[4], (D, HS), 0.02), 'w2': g(ks[5], (HS, D), 0.02), 'W1e': g(ks[6], (E, D, HE), 0.02), 'W2e': g(ks[7], (E, HE, D), 0.02)}
    _L0_cond_all = _L0_cond_setup()
    _L0_cond_in = {k: v for k, v in _L0_cond_all.items() if k in ('router_W', 'router_bias', 'w1', 'w3', 'w2', 'W1e', 'W2e')}
    del _L0_cond_all

    def _L1_cond_setup():
        import jax, jax.numpy as jnp
        import numpy as np
        B, T, C = (64, 128, 256)
        key = jax.random.key(seed)
        ks = jax.random.split(key, 17)
        s_in = 1.0 / np.sqrt(C)

        def lin(kw, kb, fan_in):
            s = 1.0 / np.sqrt(fan_in)
            W = jax.random.uniform(kw, (C, fan_in), jnp.float32, -s, s)
            b = jax.random.uniform(kb, (C,), jnp.float32, -s, s)
            return (W, b)
        Wxz, bxz = lin(ks[0], ks[1], C)
        Whz, bhz = lin(ks[2], ks[3], C)
        Wxr, bxr = lin(ks[4], ks[5], C)
        Whr, bhr = lin(ks[6], ks[7], C)
        Wxh, bxh = lin(ks[8], ks[9], C)
        Whh, bhh = lin(ks[10], ks[11], C)
        Whq, bhq = lin(ks[12], ks[13], C)
        X = jax.random.normal(ks[14], (B, T, C), jnp.float32)
        h0 = jax.random.normal(ks[15], (B, C), jnp.float32)
        return {'X': X, 'h0': h0, 'Wxz': Wxz, 'bxz': bxz, 'Whz': Whz, 'bhz': bhz, 'Wxr': Wxr, 'bxr': bxr, 'Whr': Whr, 'bhr': bhr, 'Wxh': Wxh, 'bxh': bxh, 'Whh': Whh, 'bhh': bhh, 'Whq': Whq, 'bhq': bhq}
    _L1_cond_all = _L1_cond_setup()
    _L1_cond_in = {k: v for k, v in _L1_cond_all.items() if k in ('Wxz', 'bxz', 'Whz', 'bhz', 'Wxr', 'bxr', 'Whr', 'bhr', 'Wxh', 'bxh', 'Whh', 'bhh', 'Whq', 'bhq')}
    del _L1_cond_all
    return {'x': x, 'cond_1024': cond_1024, 'L0_cond_router_W': _L0_cond_in['router_W'], 'L0_cond_router_bias': _L0_cond_in['router_bias'], 'L0_cond_w1': _L0_cond_in['w1'], 'L0_cond_w3': _L0_cond_in['w3'], 'L0_cond_w2': _L0_cond_in['w2'], 'L0_cond_W1e': _L0_cond_in['W1e'], 'L0_cond_W2e': _L0_cond_in['W2e'], 'L1_cond_Wxz': _L1_cond_in['Wxz'], 'L1_cond_bxz': _L1_cond_in['bxz'], 'L1_cond_Whz': _L1_cond_in['Whz'], 'L1_cond_bhz': _L1_cond_in['bhz'], 'L1_cond_Wxr': _L1_cond_in['Wxr'], 'L1_cond_bxr': _L1_cond_in['bxr'], 'L1_cond_Whr': _L1_cond_in['Whr'], 'L1_cond_bhr': _L1_cond_in['bhr'], 'L1_cond_Wxh': _L1_cond_in['Wxh'], 'L1_cond_bxh': _L1_cond_in['bxh'], 'L1_cond_Whh': _L1_cond_in['Whh'], 'L1_cond_bhh': _L1_cond_in['bhh'], 'L1_cond_Whq': _L1_cond_in['Whq'], 'L1_cond_bhq': _L1_cond_in['bhq']}

def reference(x, cond_1024, L0_cond_router_W, L0_cond_router_bias, L0_cond_w1, L0_cond_w3, L0_cond_w2, L0_cond_W1e, L0_cond_W2e, L1_cond_Wxz, L1_cond_bxz, L1_cond_Whz, L1_cond_bhz, L1_cond_Wxr, L1_cond_bxr, L1_cond_Whr, L1_cond_bhr, L1_cond_Wxh, L1_cond_bxh, L1_cond_Whh, L1_cond_bhh, L1_cond_Whq, L1_cond_bhq):
    import jax
    import jax.numpy as jnp

    def _L0_cond_ref(x, t_emb, router_W, router_bias, w1, w3, w2, W1e, W2e):
        import jax, jax.numpy as jnp
        import numpy as np
        D, HS, HE, E, K = (256, 512, 256, 8, 2)
        B, T = (4, 256)
        N_SHARED = 1
        Bb, Tt, C = x.shape
        xf = x.reshape(-1, C)
        tf = jnp.broadcast_to(t_emb[:, None, :], (Bb, Tt, C)).reshape(-1, C)
        N = xf.shape[0]
        shared = jax.nn.silu(xf @ w1) * (xf @ w3) @ w2
        s = jax.nn.sigmoid((jnp.concatenate([xf, tf], axis=-1) @ router_W).astype(jnp.float32))
        sel_scores = s + router_bias
        _, topk_idx = jax.lax.top_k(sel_scores, K)
        s_sel = jnp.take_along_axis(s, topk_idx, axis=1)
        denom = s_sel.sum(axis=1, keepdims=True)
        gates = jnp.where(denom > 1e-09, s_sel / (denom + 1e-09), 1.0 / K).astype(x.dtype)
        combine = jnp.zeros((N, E), x.dtype).at[jnp.arange(N)[:, None], topk_idx].add(gates)
        h = jax.nn.gelu(jnp.einsum('nc,ech->enh', xf, W1e), approximate=False)
        y = jnp.einsum('enh,ehc->enc', h, W2e)
        routed = jnp.einsum('ne,enc->nc', combine, y)
        return ((shared + routed) / (N_SHARED + K)).reshape(Bb, Tt, C)

    def _L1_cond_ref(X, h0, Wxz, bxz, Whz, bhz, Wxr, bxr, Whr, bhr, Wxh, bxh, Whh, bhh, Whq, bhq):
        import jax, jax.numpy as jnp
        import numpy as np
        B, T, C = (64, 128, 256)
        Xz = jnp.einsum('btc,hc->tbh', X, Wxz) + bxz
        Xr = jnp.einsum('btc,hc->tbh', X, Wxr) + bxr
        Xh = jnp.einsum('btc,hc->tbh', X, Wxh) + bxh

        def step(H, xs):
            xz, xr, xh = xs
            Z = jax.nn.sigmoid(xz + H @ Whz.T + bhz)
            R = jax.nn.sigmoid(xr + H @ Whr.T + bhr)
            H_tilda = jnp.tanh(xh + R * H @ Whh.T + bhh)
            H_new = Z * H + (1.0 - Z) * H_tilda
            Y = H_new @ Whq.T + bhq
            return (H_new, Y)
        _, Ys = jax.lax.scan(step, h0, (Xz, Xr, Xh))
        return jnp.transpose(Ys, (1, 0, 2))
    x = x + _L0_cond_ref(x, cond_1024, L0_cond_router_W, L0_cond_router_bias, L0_cond_w1, L0_cond_w3, L0_cond_w2, L0_cond_W1e, L0_cond_W2e)
    x = x + _L1_cond_ref(x, cond_1024, L1_cond_Wxz, L1_cond_bxz, L1_cond_Whz, L1_cond_bhz, L1_cond_Wxr, L1_cond_bxr, L1_cond_Whr, L1_cond_bhr, L1_cond_Wxh, L1_cond_bxh, L1_cond_Whh, L1_cond_bhh, L1_cond_Whq, L1_cond_bhq)
    return x

_drawn_inputs = setup_inputs


def setup_inputs(seed=0):
    import zlib

    import numpy as np

    out = dict(_drawn_inputs(seed))
    spreads = {'L0_cond_router_bias': (0.0, 0.554)}
    factors = {'cond_1024': 2.983,
     'L0_cond_router_W': 8.0,
     'L0_cond_w1': 7.149,
     'L0_cond_w3': 7.03,
     'L0_cond_w2': 7.05,
     'L0_cond_W1e': 4.449,
     'L0_cond_W2e': 4.341,
     'L1_cond_bxz': 47.982,
     'L1_cond_Whz': 4.074,
     'L1_cond_bhz': 52.178,
     'L1_cond_Wxr': 40.356,
     'L1_cond_bxr': 64.0,
     'L1_cond_Whr': 64.0,
     'L1_cond_bhr': 64.0,
     'L1_cond_bxh': 20.631,
     'L1_cond_bhh': 21.956,
     'L1_cond_Whh': 3.397,
     'L1_cond_bhq': 5.762}
    for name, (base, spread) in spreads.items():
        noise = np.random.default_rng([zlib.crc32(name.encode()), seed]).standard_normal(out[name].shape)
        drawn = base * np.exp(spread * noise) if base else spread * noise
        out[name] = jnp.asarray(drawn.astype(out[name].dtype))
    for name, factor in factors.items():
        out[name] = (out[name] * factor).astype(out[name].dtype)
    return out
```

```python
import concourse.bass as bass
from concourse import mybir
from contextlib import ExitStack



def moe_then_gru(nc, x, cond, router_w, router_b, w1, w3, w2, we1, we2,
                 wxz, bxz, whz, bhz, wxr, bxr, whr, bhr, wxh, bxh, whh, bhh, whq, bhq, out):
    F32 = mybir.dt.float32
    ALU = mybir.AluOpType
    ACT = mybir.ActivationFunctionType
    AX = mybir.AxisListType

    B, T, C = x.shape
    P = 128
    TS = P // B
    NT = T // TS
    KC = C // P
    HS = w1.shape[1]
    NE = we1.shape[0]
    HE = we1.shape[2]
    NSH = HS // P
    NUP = NSH + NE
    NDN = 1 + NE
    NG = 4
    GW = C // NG
    Q = 32
    NI = GW // Q
    GATES = 3
    RW = GATES * GW
    TOP_K = 2
    HALF = TS // 2

    ctx = ExitStack()
    with ctx:
        def sb(name, shape):
            return ctx.enter_context(nc.sbuf_tensor(name, shape, F32))

        def sem(name):
            return ctx.enter_context(nc.semaphore(name))

        x_all = sb("x_all", [P, NT, C])
        xT_all = sb("xT_all", [P, NT, KC, P])
        cond_tok = sb("cond_tok", [P, C])
        condT = sb("condT", [P, KC, P])
        rw_sb = sb("rw_sb", [P, 2 * KC, NE])
        rbias = sb("rbias", [P, NE])
        w1_sb = sb("w1_sb", [P, KC, HS])
        w3_sb = sb("w3_sb", [P, KC, HS])
        w2_sb = sb("w2_sb", [P, NSH, C])
        we1_sb = sb("we1_sb", [P, NE, KC, HE])
        we2_sb = sb("we2_sb", [P, NE, HE // P, C])
        raw = [sb(f"raw{i}", [P, KC, C]) for i in range(7)]
        ordered = {r: sb(f"ordered{r}", [P, KC, C]) for r in (1, 3, 5, 6)}
        wxT = sb("wxT", [P, KC, NG, GATES, GW])
        whT = sb("whT", [P, GATES, NI, C])
        wqT = sb("wqT", [P, NI, C])
        bias_x = sb("bias_x", [P, NG, GATES, GW])
        bias_h = sb("bias_h", [P, NG, GATES, GW])
        bias_q = sb("bias_q", [P, C])
        ident = sb("ident", [P, P])
        zeros = sb("zeros", [P, RW])
        rank = sb("rank", [P, NE])
        logits = sb("logits", [P, NT, NE])
        rbase = sb("rbase", [P, NE])
        score = sb("score", [P, NT, NE])
        sel = sb("sel", [P, NT, NE])
        hit = sb("hit", [P, NT, NE])
        first = sb("first", [P, NT, NE])
        mask = sb("mask", [P, NT, NE])
        gates_all = sb("gates_all", [P, NT, NE])
        best = sb("best", [P, NT])
        den = sb("den", [P, NT])
        rden = sb("rden", [P, NT])
        okay = sb("okay", [P, NT])
        xT_cur = sb("xT_cur", [P, KC, P])
        x_cur = sb("x_cur", [P, C])
        gates_cur = sb("gates_cur", [P, NE])
        sig = sb("sig", [P, 2, P])
        silu = sb("silu", [P, 2, P])
        hid = sb("hid", [P, NUP, 2 * P])
        acc = sb("acc", [P, C])
        x1_cur = sb("x1_cur", [P, C])
        x1T = sb("x1T", [P, KC, P])
        xproj = sb("xproj", [P, NG, RW])
        xs = sb("xs", [P, TS, RW])
        state = sb("state", [P, 2, GW])
        h0_rows = sb("h0_rows", [P, GW])
        t_r = sb("t_r", [P, GW])
        t_z = sb("t_z", [P, GW])
        t_h = sb("t_h", [P, GW])
        rh = sb("rh", [P, GW])
        rhT = sb("rhT", [P, GW])
        zs = sb("zs", [P, GW])
        cand = sb("cand", [P, GW])
        hist = sb("hist", [P, TS, NI, Q])
        yst = sb("yst", [P, NI, P])
        x_res = sb("x_res", [P, C])
        y_bias = sb("y_bias", [P, C])
        y_out = sb("y_out", [P, C])

        bank = [ctx.enter_context(nc.psum_tensor(f"bank{i}", [P, 512], F32)) for i in range(8)]
        r_ps, zc_ps = bank[0], bank[1]
        up_ps = bank[2:4]
        dn_ps = bank[4:6]
        xp_ps = bank[6]
        misc = bank[7]
        tr_ps = bank[2:6]

        by_token = nc.dram_tensor("gate_inputs_by_token", [P, NG, RW], F32, kind="Internal").ap()

        ld_x = sem("ld_x")
        ld_router = sem("ld_router")
        ld_gru = sem("ld_gru")
        ld_bias = sem("ld_bias")
        ld_w13 = sem("ld_w13")
        ld_w2 = sem("ld_w2")
        ld_we1 = sem("ld_we1")
        ld_we2 = sem("ld_we2")
        ident0 = sem("ident0")
        ident_ready = sem("ident_ready")
        consts_ready = sem("consts_ready")
        ordered_done = sem("ordered_done")
        tr_done = sem("tr_done")
        tr_act = sem("tr_act")
        tr_dve = sem("tr_dve")
        logits_done = sem("logits_done")
        logits_ready = sem("logits_ready")
        score_ready = sem("score_ready")
        gates_ready = sem("gates_ready")
        dve_setup = sem("dve_setup")
        bias_ready = sem("bias_ready")
        xT_loaded = sem("xT_loaded")
        xg_loaded = sem("xg_loaded")
        up_done = sem("up_done")
        sig_done = sem("sig_done")
        silu_done = sem("silu_done")
        shared_ready = sem("shared_ready")
        gelu_ready = sem("gelu_ready")
        dn_done = sem("dn_done")
        acc_done = sem("acc_done")
        x1_done = sem("x1_done")
        x1_stored = sem("x1_stored")
        x1T_done = sem("x1T_done")
        x1T_ready = sem("x1T_ready")
        xp_done = sem("xp_done")
        xp_ready = sem("xp_ready")
        xp_stored = sem("xp_stored")
        xs_first = sem("xs_first")
        xs_second = sem("xs_second")
        bits_set = sem("bits_set")
        seeded_r = sem("seeded_r")
        seeded_zc = sem("seeded_zc")
        hT_ready = sem("hT_ready")
        r_done = sem("r_done")
        z_done = sem("z_done")
        c_done = sem("c_done")
        tr_ready = sem("tr_ready")
        tz_ready = sem("tz_ready")
        th_ready = sem("th_ready")
        rh_done = sem("rh_done")
        rhT_ready = sem("rhT_ready")
        zs_done = sem("zs_done")
        cand_done = sem("cand_done")
        state_done = sem("state_done")
        yst_ready = sem("yst_ready")
        y_done = sem("y_done")
        x_res_loaded = sem("x_res_loaded")
        y_bias_done = sem("y_bias_done")
        y_ready = sem("y_ready")
        out_stored = sem("out_stored")

        XG = NT * KC // 4
        WORDER = [(0, "x", 0), (2, "x", 1), (4, "x", 2), (1, "h", 0), (3, "h", 1), (5, "h", 2), (6, "q", 0)]
        WSCALE = {"x": [1.0, 1.0, 1.0], "h": [0.5, 0.5, 0.25], "q": [0.5]}
        WGROUPS = [(r, kind, gate, k) for r, kind, gate in WORDER for k in range(KC)]
        NTR = XG + 1 + len(WGROUPS)
        gru_w = [wxr, whr, wxz, whz, wxh, whh, whq]
        gate_bx = [bxr, bxz, bxh]
        gate_bh = [bhr, bhz, bhh]
        LDX, LDR, LDG = 16 * B, 16 * (2 + B), 16 * (7 + NG)
        LDB = 16 * (2 * GATES * 1 + 1)

        def evacuate(m):
            src = tr_ps[m % 4]
            if m < XG:
                n = 4 // KC
                return xT_all[:, m * n:(m + 1) * n, :, :].rearrange("p n k t -> p (n k t)"), src[:, 0:512], 1.0
            if m == XG:
                return condT[:, :, :].rearrange("p k t -> p (k t)"), src[:, 0:C], 1.0
            _, kind, gate, k = WGROUPS[m - XG - 1]
            s = WSCALE[kind][gate]
            if kind == "x":
                return wxT[:, k, :, gate, :], src[:, 0:C].rearrange("p (j n) -> p j n", j=NG), s
            if kind == "h":
                return whT[:, gate, k, :], src[:, 0:C], s
            return wqT[:, k, :], src[:, 0:C], s

        def up_unit(s):
            return s if s < NUP else None

        XP_STEP = 2
        Y_STEP = XP_STEP + 2 * GATES
        DN_STEP = Y_STEP + NI
        DN_GAP1 = {DN_STEP: ["s0", "s1"], DN_STEP + 1: ["s2", "s3"], 12: [0], 13: [2], 14: [4], 15: [6]}
        DN_GAP2 = {12: [1], 13: [3], 14: [5], 15: [7]}

        def stages(n):
            return 0 <= n < NT, n + 2 < NT, 0 <= n + 1 < NT, 0 <= n - 1 < NT

        def iterations(eng, body):
            for n in (-2, -1, 0, 1):
                body(n, *stages(n), n + 3 < NT)
            with eng.Fori(2, NT - 3) as i:
                body(i, True, True, True, True, True)
            for n in range(NT - 3, NT + 1):
                body(n, *stages(n), n + 3 < NT)

        def above(n, least):
            return n >= least if isinstance(n, int) else True

        block = ctx.enter_context(nc.Block())

        @block.sync
        def _(sp):
            for b in range(B):
                sp.dma_start(x_all[b * TS:(b + 1) * TS, :, :],
                             x[b, :, :].rearrange("(n t) c -> t n c", t=TS)).then_inc(ld_x, 16)
            sp.dma_start(rw_sb[:, :, :], router_w.rearrange("(k p) e -> p k e", p=P)).then_inc(ld_router, 16)
            sp.dma_start(rbias[:, :], router_b.rearrange("(a e) -> a e", a=1).to_broadcast([P, NE])).then_inc(ld_router, 16)
            for b in range(B):
                sp.dma_start(cond_tok[b * TS:(b + 1) * TS, :],
                             cond[b:b + 1, :].to_broadcast([TS, C])).then_inc(ld_router, 16)
            for r in range(7):
                sp.dma_start(raw[r][:, :, :], gru_w[r].rearrange("(o p) c -> p o c", p=P)).then_inc(ld_gru, 16)
            sp.wait_ge(consts_ready, 1)
            for j in range(NG):
                sp.dma_start(h0_rows[Q * j:Q * j + B, :], cond[:, GW * j:GW * (j + 1)]).then_inc(ld_gru, 16)
            sp.dma_start(w1_sb[:, :, :], w1.rearrange("(k p) h -> p k h", p=P)).then_inc(ld_w13, 16)
            sp.dma_start(w3_sb[:, :, :], w3.rearrange("(k p) h -> p k h", p=P)).then_inc(ld_w13, 16)
            sp.dma_start(we1_sb[:, :, :, :], we1.rearrange("e (k p) h -> p e k h", p=P)).then_inc(ld_we1, 16)
            sp.dma_start(w2_sb[:, :, :], w2.rearrange("(k p) c -> p k c", p=P)).then_inc(ld_w2, 16)
            sp.dma_start(we2_sb[:, :, :, :], we2.rearrange("e (k p) c -> p e k c", p=P)).then_inc(ld_we2, 16)
            for gate in range(GATES):
                for dst, src in ((bias_x, gate_bx[gate]), (bias_h, gate_bh[gate])):
                    sp.dma_start(dst[:, :, gate, :], src.rearrange("(a j n) -> a j n", a=1, j=NG)
                                 .to_broadcast([P, NG, GW])).then_inc(ld_bias, 16)
            sp.dma_start(bias_q[:, :], bhq.rearrange("(a c) -> a c", a=1).to_broadcast([P, C])).then_inc(ld_bias, 16)
            sp.wait_ge(tr_act, 1)
            sp.dma_start(xT_cur[:, :, :], xT_all[:, 0, :, :]).then_inc(xT_loaded, 16)

            def gate_rows(half, done):
                for j in range(NG):
                    src = by_token[:, j, :].rearrange("(b t) c -> b t c", b=B)[:, half * HALF:(half + 1) * HALF, :]
                    sp.dma_start(xs[Q * j:Q * j + B, half * HALF:(half + 1) * HALF, :], src).then_inc(done, 16)

            def body(n, scan, moe, proj, outs, more):
                if moe:
                    if above(n, -1):
                        sp.wait_ge(x1_done, n + 2)
                    sp.wait_ge(gates_ready, 1)
                    sp.dma_start(x_cur[:, :], x_all[:, bass.ds(n + 2, 1), :].rearrange("p a c -> p (a c)")).then_inc(xg_loaded, 16)
                    sp.dma_start(gates_cur[:, :], gates_all[:, bass.ds(n + 2, 1), :].rearrange("p a c -> p (a c)")).then_inc(xg_loaded, 16)
                if proj:
                    sp.wait_ge(x1_done, n + 2)
                    sp.dma_start(x_all[:, bass.ds(n + 1, 1), :].rearrange("p a c -> p (a c)"), x1_cur[:, :]).then_inc(x1_stored, 16)
                if outs:
                    if above(n, 2):
                        sp.wait_ge(y_ready, n - 1)
                    if not proj:
                        sp.wait_ge(x1_stored, 16 * n)
                    sp.dma_start(x_res[:, :], x_all[:, bass.ds(n - 1, 1), :].rearrange("p a c -> p (a c)")).then_inc(x_res_loaded, 16)
                if proj:
                    sp.wait_ge(xp_ready, GATES * (n + 2))
                    sp.dma_start(by_token, xproj[:, :, :]).then_inc(xp_stored, 16)
                    sp.wait_ge(xp_stored, 16 * (n + 2))
                    gate_rows(0, xs_first)
                if outs:
                    sp.wait_ge(y_ready, n)
                    sp.dma_start(out_tile(n - 1), y_out[:, :]).then_inc(out_stored, 16)
                if more:
                    sp.wait_ge(up_done, NUP * (n + 3))
                    sp.dma_start(xT_cur[:, :, :], xT_all[:, bass.ds(n + 3, 1), :, :].rearrange("p a k t -> p (a k) t")).then_inc(xT_loaded, 16)
                if proj:
                    if scan:
                        sp.wait_ge(seeded_zc, TS * (n + 1))
                    gate_rows(1, xs_second)

            def out_tile(n):
                return out[:, bass.ds(n * TS, TS), :]

            iterations(sp, body)
            sp.wait_ge(out_stored, 16 * NT)

        @block.gpsimd
        def _(pool):
            pool.memset(h0_rows[:, :], 0.0).then_inc(ident0, 1)
            pool.memset(ident[:, :], 0.0).then_inc(ident0, 1)
            pool.wait_ge(ident0, 2)
            pool.affine_select(out=ident[:, :], in_=ident[:, :], compare_op=ALU.not_equal, fill=1.0, base=0,
                               pattern=[[-1, P]], channel_multiplier=1).then_inc(ident_ready, 1)
            for e in range(NE):
                pool.memset(rank[:, e:e + 1], float(NE - e)).then_inc(ident0, 1)
            pool.memset(zeros[:, :], 0.0).then_inc(ident0, 1)
            pool.memset(xs[:, :, :], 0.0).then_inc(ident0, 1)
            pool.wait_ge(ident0, 2 + NE + 2)
            pool.drain().then_inc(consts_ready, 1)

            pool.wait_ge(ld_gru, LDG)
            for r, w in ordered.items():
                for o in range(KC):
                    pool.tensor_copy(w[:, o, :].rearrange("p (i j c) -> p i j c", i=NI, j=NG),
                                     raw[r][:, o, :].rearrange("p (j i c) -> p i j c", j=NG, i=NI)).then_inc(ordered_done, 1)

        @block.scalar
        def _(act):
            for m in range(0, NTR, 2):
                act.wait_ge(tr_done, m + 1)
                dst, src, s = evacuate(m)
                act.activation(dst, src, ACT.Copy, scale=s).then_inc(tr_act, 1)
            act.wait_ge(logits_ready, 1)
            act.activation(score[:, :, :], logits[:, :, :], ACT.Sigmoid).then_inc(score_ready, 1)

            def consume_up(n, u):
                ps = up_ps[u % 2]
                act.wait_ge(up_done, NUP * (n + 2) + u + 1)
                if u < NSH:
                    act.activation(sig[:, u % 2, :], ps[:, 0:P], ACT.Tanh, scale=0.5).then_inc(sig_done, 1)
                else:
                    act.activation(hid[:, u, :], ps[:, 0:2 * P], ACT.Gelu).then_inc(gelu_ready, 1)

            def seed(n, s, ps, cols, used, done):
                if s == 0:
                    act.wait_ge(xs_first, 16 * NG * (n + 1))
                if s == HALF:
                    act.wait_ge(xs_second, 16 * NG * (n + 1))
                if isinstance(n, int) and n == 0 and s == 0:
                    act.wait_ge(bits_set, 2)
                    act.wait_ge(consts_ready, 1)
                else:
                    act.wait_ge(used, TS * n + s)
                act.activation(ps[:, 0:cols.stop - cols.start], xs[:, s, cols], ACT.Copy).then_inc(done, 1)

            def seed_r(n, s):
                seed(n, s, r_ps, slice(0, GW), tr_ready, seeded_r)

            def seed_zc(n, s):
                seed(n, s, zc_ps, slice(GW, RW), th_ready, seeded_zc)

            def body(n, scan, moe, proj, outs, more):
                for s in range(TS):
                    after = (n, s + 1) if s + 1 < TS and scan else (n + 1, 0) if s + 1 == TS and proj else None
                    if scan:
                        act.wait_ge(r_done, TS * n + s + 1)
                        act.activation(t_r[:, :], r_ps[:, 0:GW], ACT.Tanh, scale=0.5).then_inc(tr_ready, 1)
                    if after:
                        seed_r(*after)
                    if scan:
                        act.wait_ge(z_done, TS * n + s + 1)
                        act.activation(t_z[:, :], zc_ps[:, 0:GW], ACT.Tanh, scale=0.5).then_inc(tz_ready, 1)
                    if outs and s == 0:
                        act.wait_ge(hT_ready, TS * n + 1)
                        if above(n, 2):
                            act.wait_ge(y_done, n - 1)
                        act.activation(yst[:, :, :].rearrange("p i (b t) -> p i b t", b=B),
                                       hist[:, :, :, 0:B].rearrange("p t i b -> p i b t"), ACT.Copy).then_inc(yst_ready, 1)
                    if moe and s >= 1 and up_unit(s - 1) is not None:
                        consume_up(n, s - 1)
                    if scan:
                        act.wait_ge(c_done, TS * n + s + 1)
                        act.activation(t_h[:, :], zc_ps[:, GW:2 * GW], ACT.Tanh).then_inc(th_ready, 1)
                    if after:
                        seed_zc(*after)
                    if proj and s == XP_STEP - 1:
                        act.wait_ge(x1T_done, n + 2)
                        act.activation(x1T[:, :, :].rearrange("p k t -> p (k t)"), misc[:, 0:C], ACT.Copy)\
                           .then_inc(x1T_ready, 1)

            iterations(act, body)

        @block.vector
        def _(dve):
            chain = [0]

            def link(ins):
                chain[0] += 1
                ins.then_inc(dve_setup, 1)
                dve.wait_ge(dve_setup, chain[0])

            for m in range(1, NTR, 2):
                dve.wait_ge(tr_done, m + 1)
                dst, src, s = evacuate(m)
                dve.tensor_scalar(dst, src, s, None, ALU.mult).then_inc(tr_dve, 1)

            dve.wait_ge(ld_router, LDR)
            dve.wait_ge(consts_ready, 1)
            dve.wait_ge(logits_done, 1)
            over_tiles = lambda a: a.rearrange("p (a e) -> p a e", a=1).to_broadcast([P, NT, NE])
            over_experts = lambda a: a.rearrange("p (n a) -> p n a", a=1).to_broadcast([P, NT, NE])
            link(dve.tensor_copy(rbase[:, :], misc[:, NT * NE:(NT + 1) * NE]))
            dve.tensor_tensor(logits[:, :, :], misc[:, 0:NT * NE].rearrange("p (n e) -> p n e", e=NE),
                              over_tiles(rbase[:, :]), ALU.add).then_inc(logits_ready, 1)
            dve.wait_ge(score_ready, 1)
            link(dve.tensor_tensor(sel[:, :, :], score[:, :, :], over_tiles(rbias[:, :]), ALU.add))
            for k in range(TOP_K):
                link(dve.tensor_reduce(best[:, :], sel[:, :, :], AX.X, ALU.max))
                link(dve.tensor_tensor(hit[:, :, :], sel[:, :, :], over_experts(best[:, :]), ALU.is_equal))
                link(dve.tensor_tensor(hit[:, :, :], hit[:, :, :], over_tiles(rank[:, :]), ALU.mult))
                link(dve.tensor_reduce(best[:, :], hit[:, :, :], AX.X, ALU.max))
                link(dve.tensor_tensor(first[:, :, :], hit[:, :, :], over_experts(best[:, :]), ALU.is_equal))
                if k == 0:
                    link(dve.tensor_copy(mask[:, :, :], first[:, :, :]))
                    link(dve.scalar_tensor_tensor(sel[:, :, :], first[:, :, :], -1e30, sel[:, :, :], ALU.mult, ALU.add))
                else:
                    link(dve.tensor_tensor(mask[:, :, :], mask[:, :, :], first[:, :, :], ALU.add))
            link(dve.tensor_tensor(score[:, :, :], score[:, :, :], mask[:, :, :], ALU.mult))
            link(dve.tensor_reduce(den[:, :], score[:, :, :], AX.X, ALU.add))
            link(dve.tensor_scalar(okay[:, :], den[:, :], 1e-9, None, ALU.is_gt))
            link(dve.tensor_scalar(rden[:, :], den[:, :], 1e-9, None, ALU.add))
            link(dve.reciprocal(rden[:, :], rden[:, :]))
            link(dve.tensor_tensor(rden[:, :], rden[:, :], okay[:, :], ALU.mult))
            link(dve.tensor_scalar(okay[:, :], okay[:, :], -1.0 / TOP_K, 1.0 / TOP_K, ALU.mult, ALU.add))
            link(dve.tensor_tensor(score[:, :, :], score[:, :, :], over_experts(rden[:, :]), ALU.mult))
            link(dve.tensor_tensor(mask[:, :, :], mask[:, :, :], over_experts(okay[:, :]), ALU.mult))
            dve.tensor_tensor(gates_all[:, :, :], score[:, :, :], mask[:, :, :], ALU.add).then_inc(gates_ready, 1)
            dve.wait_ge(ld_bias, LDB)
            dve.tensor_tensor(bias_x[:, :, :, :], bias_x[:, :, :, :], bias_h[:, :, :, :], ALU.add).then_inc(bias_ready, 1)
            dve.wait_ge(ld_gru, LDG)
            dve.tensor_scalar(state[:, 0, :], h0_rows[:, :], 2.0, None, ALU.mult).then_inc(state_done, 1)
            dve.wait_ge(state_done, 1)
            dve.transpose(hist[:, TS - 1, :, :].rearrange("p i q -> p (i q)"), state[:, 0, :]).then_inc(hT_ready, 1)

            def shared_hidden(n, u):
                ps = up_ps[u % 2]
                dve.wait_ge(sig_done, NSH * (n + 2) + u + 1)
                dve.scalar_tensor_tensor(silu[:, u % 2, :], sig[:, u % 2, :], 1.0, ps[:, 0:P], ALU.add, ALU.mult)\
                   .then_inc(silu_done, 1)
                dve.wait_ge(silu_done, NSH * (n + 2) + u + 1)
                dve.tensor_tensor(hid[:, u, 0:P], silu[:, u % 2, :], ps[:, P:2 * P], ALU.mult).then_inc(shared_ready, 1)

            def accumulate(n, g):
                ps = dn_ps[g % 2]
                dve.wait_ge(dn_done, NDN * (n + 2) + g + 1)
                if g == 0:
                    if above(n, -1):
                        dve.wait_ge(x1_done, n + 2)
                    dve.tensor_scalar(acc[:, :], ps[:, 0:C], 0.5, None, ALU.mult).then_inc(acc_done, 1)
                    return
                if g == 1:
                    dve.wait_ge(xg_loaded, 32 * (n + 3))
                dve.wait_ge(acc_done, NDN * (n + 2) + g)
                dve.scalar_tensor_tensor(acc[:, :], ps[:, 0:C], gates_cur[:, g - 1:g], acc[:, :],
                                         ALU.mult, ALU.add).then_inc(acc_done, 1)

            def finish_x1(n):
                dve.wait_ge(acc_done, NDN * (n + 2))
                if above(n, 0):
                    dve.wait_ge(x1T_done, n + 1)
                    dve.wait_ge(x1_stored, 16 * (n + 1))
                dve.scalar_tensor_tensor(x1_cur[:, :], acc[:, :], 1.0 / (1 + TOP_K), x_cur[:, :],
                                         ALU.mult, ALU.add).then_inc(x1_done, 1)

            def add_bias(n, q):
                dve.wait_ge(xp_done, GATES * (n + 1) + q + 1)
                if isinstance(n, int) and n == -1:
                    dve.wait_ge(bias_ready, 1)
                else:
                    dve.wait_ge(xp_stored, 16 * (n + 1))
                    dve.wait_ge(xs_second, 16 * NG * (n + 1))
                    if q == GATES - 1:
                        dve.wait_ge(seeded_zc, TS * n + HALF)
                cols = slice(q * C, (q + 1) * C)
                dve.tensor_tensor(xproj[:, :, :].rearrange("p j c -> p (j c)")[:, cols],
                                  xp_ps[:, 0:C],
                                  bias_x[:, :, :, :].rearrange("p j g c -> p (j g c)")[:, cols],
                                  ALU.add).then_inc(xp_ready, 1)

            def finish_out(n):
                dve.wait_ge(y_done, n)
                if above(n, 2):
                    dve.wait_ge(y_ready, n - 1)
                dve.tensor_tensor(y_bias[:, :], misc[:, C:2 * C], bias_q[:, :], ALU.add).then_inc(y_bias_done, 1)
                dve.wait_ge(y_bias_done, n)
                dve.wait_ge(x_res_loaded, 16 * n)
                if above(n, 2):
                    dve.wait_ge(out_stored, 16 * (n - 1))
                dve.tensor_tensor(y_out[:, :], y_bias[:, :], x_res[:, :], ALU.add).then_inc(y_ready, 1)

            def body(n, scan, moe, proj, outs, more):
                for s in range(TS):
                    old, new = state[:, s % 2, :], state[:, (s + 1) % 2, :]
                    if scan:
                        dve.wait_ge(state_done, TS * n + s + 1)
                        dve.wait_ge(tr_ready, TS * n + s + 1)
                        dve.scalar_tensor_tensor(rh[:, :], t_r[:, :], 1.0, old, ALU.add, ALU.mult).then_inc(rh_done, 1)
                        dve.wait_ge(rh_done, TS * n + s + 1)
                        dve.transpose(rhT[:, :], rh[:, :]).then_inc(rhT_ready, 1)
                        dve.wait_ge(tz_ready, TS * n + s + 1)
                        dve.scalar_tensor_tensor(zs[:, :], t_z[:, :], 1.0, old, ALU.add, ALU.mult).then_inc(zs_done, 1)
                    if s == 0 and proj:
                        accumulate(n - 1, NDN - 1)
                        finish_x1(n)
                    if moe and s in DN_GAP2 and s - 1 in DN_GAP2:
                        accumulate(n, 1 + DN_GAP2[s - 1][0])
                    if scan:
                        dve.wait_ge(th_ready, TS * n + s + 1)
                        dve.scalar_tensor_tensor(cand[:, :], t_z[:, :], -1.0, t_h[:, :], ALU.add, ALU.mult)\
                           .then_inc(cand_done, 1)
                        dve.wait_ge(zs_done, TS * n + s + 1)
                        dve.wait_ge(cand_done, TS * n + s + 1)
                        dve.scalar_tensor_tensor(new, zs[:, :], 0.5, cand[:, :], ALU.mult, ALU.subtract)\
                           .then_inc(state_done, 1)
                        if s == 0 and outs:
                            dve.wait_ge(yst_ready, n)
                        dve.wait_ge(state_done, TS * n + s + 2)
                        dve.transpose(hist[:, s, :, :].rearrange("p i q -> p (i q)"), new).then_inc(hT_ready, 1)
                    if moe and 1 <= s <= NSH:
                        shared_hidden(n, s - 1)
                    if proj and s >= XP_STEP and (s - XP_STEP) % 2 == 1 and s < Y_STEP:
                        add_bias(n, (s - XP_STEP) // 2)
                    if outs and s == DN_STEP - 1:
                        finish_out(n)
                    if moe and s == DN_STEP + 1:
                        accumulate(n, 0)
                    if moe and s in DN_GAP2:
                        accumulate(n, 1 + DN_GAP1[s][0])

            iterations(dve, body)

        @block.tensor
        def _(pe):
            pe.wait_ge(ident_ready, 1)
            pe.wait_ge(consts_ready, 1)
            for p in (r_ps, zc_ps):
                pe.matmul(p[:, 0:2 * GW], zeros[:, 0:P], zeros[:, 0:2 * GW], start=True, stop=True).then_inc(bits_set, 1)

            def transposes(m):
                if m >= 4:
                    pe.wait_ge(tr_act if m % 2 == 0 else tr_dve, (m - 4) // 2 + 1)
                dst = tr_ps[m % 4]
                if m < XG:
                    blocks = [x_all[:, (4 * m + i) // KC, ((4 * m + i) % KC) * P:((4 * m + i) % KC + 1) * P] for i in range(4)]
                elif m == XG:
                    blocks = [cond_tok[:, k * P:(k + 1) * P] for k in range(KC)]
                else:
                    r, kind, gate, k = WGROUPS[m - XG - 1]
                    blocks = [(raw[r] if kind == "x" else ordered[r])[:, o, k * P:(k + 1) * P] for o in range(KC)]
                for i, blk in enumerate(blocks):
                    last = pe.transpose(dst[:, i * P:(i + 1) * P], blk, ident[:, :])
                last.then_inc(tr_done, 1)

            pe.wait_ge(ld_x, LDX)
            for m in range(XG):
                transposes(m)
            pe.wait_ge(ld_router, LDR)
            transposes(XG)
            pe.wait_ge(ld_gru, LDG)
            pe.wait_ge(ordered_done, len(ordered) * KC)
            for m in range(XG + 1, NTR):
                transposes(m)
            pe.wait_ge(tr_act, XG // 2 + 1)
            pe.wait_ge(tr_dve, XG // 2)
            for k in range(KC):
                pe.matmul(misc[:, NT * NE:(NT + 1) * NE], condT[:, k, :], rw_sb[:, KC + k, :], start=(k == 0), stop=(k == KC - 1))
            for n in range(NT):
                for k in range(KC):
                    last = pe.matmul(misc[:, n * NE:(n + 1) * NE], xT_all[:, n, k, :], rw_sb[:, k, :],
                                     start=(k == 0), stop=(k == KC - 1))
            last.then_inc(logits_done, 1)
            pe.wait_ge(tr_act, (NTR + 1) // 2)
            pe.wait_ge(tr_dve, NTR // 2)

            def up(n, u, half):
                if half == 0:
                    if u == 0:
                        pe.wait_ge(xT_loaded, 16 * (n + 3))
                    if u < 2:
                        if above(n, -1):
                            pe.wait_ge(gelu_ready, NE * (n + 2) + u - 1)
                    elif u - 2 < NSH:
                        pe.wait_ge(shared_ready, NSH * (n + 2) + u - 1)
                    else:
                        pe.wait_ge(gelu_ready, NE * (n + 2) + u - 1 - NSH)
                dst = up_ps[u % 2][:, half * P:(half + 1) * P]
                for k in range(KC):
                    if u < NSH:
                        w = (w1_sb, w3_sb)[half][:, k, u * P:(u + 1) * P]
                    else:
                        w = we1_sb[:, u - NSH, k, half * P:(half + 1) * P]
                    last = pe.matmul(dst, w, xT_cur[:, k, :], start=(k == 0), stop=(k == KC - 1))
                if half == 1:
                    last.then_inc(up_done, 1)

            def down_shared(n, u):
                if u == 0:
                    if above(n, -1):
                        pe.wait_ge(acc_done, NDN * (n + 2))
                pe.wait_ge(shared_ready, NSH * (n + 2) + u + 1)
                last = pe.matmul(dn_ps[0][:, 0:C], hid[:, u, 0:P], w2_sb[:, u, :], start=(u == 0), stop=(u == NSH - 1))
                if u == NSH - 1:
                    last.then_inc(dn_done, 1)

            def down(n, e):
                if e > 0:
                    pe.wait_ge(acc_done, NDN * (n + 2) + e)
                pe.wait_ge(gelu_ready, NE * (n + 2) + e + 1)
                for k in range(HE // P):
                    last = pe.matmul(dn_ps[(1 + e) % 2][:, 0:C], hid[:, NSH + e, k * P:(k + 1) * P], we2_sb[:, e, k, :],
                                     start=(k == 0), stop=(k == HE // P - 1))
                last.then_inc(dn_done, 1)

            def transpose_x1(n):
                pe.wait_ge(x1_done, n + 2)
                if above(n, 2):
                    pe.wait_ge(y_bias_done, n - 1)
                elif above(n, 0):
                    pe.wait_ge(x1T_ready, n + 1)
                else:
                    pe.wait_ge(logits_ready, 1)
                for k in range(KC):
                    last = pe.transpose(misc[:, k * P:(k + 1) * P], x1_cur[:, k * P:(k + 1) * P], ident[:, :])
                last.then_inc(x1T_done, 1)

            def project(n, q, k):
                if k == 0:
                    if q == 0:
                        pe.wait_ge(x1T_ready, n + 2)
                    if q > 0 or above(n, 0):
                        pe.wait_ge(xp_ready, GATES * (n + 1) + q)
                last = pe.matmul(xp_ps[:, 0:C], x1T[:, k, :],
                                 wxT[:, k, :, :, :].rearrange("p j g c -> p (j g c)")[:, q * C:(q + 1) * C],
                                 start=(k == 0), stop=(k == KC - 1))
                if k == KC - 1:
                    last.then_inc(xp_done, 1)

            def output(n, i):
                if i == 0:
                    pe.wait_ge(yst_ready, n)
                    if above(n, 2):
                        pe.wait_ge(y_bias_done, n - 1)
                last = pe.matmul(misc[:, C:2 * C], yst[:, i, :], wqT[:, i, :], start=(i == 0), stop=(i == NI - 1))
                if i == NI - 1:
                    last.then_inc(y_done, 1)

            def gate_product(ps, col, gate, lhsT):
                for i in range(NI):
                    for j in range(NG):
                        last = pe.matmul(ps[Q * j:Q * (j + 1), col:col + GW], lhsT[:, i, :],
                                         whT[:, gate, i, j * GW:(j + 1) * GW], start=False, stop=(i == NI - 1),
                                         tile_position=(0, Q * j), skip_group_check=True)
                return last

            def body(n, scan, moe, proj, outs, more):
                for s in range(TS):
                    hT = hist[:, (s - 1) % TS, :, :]
                    if scan:
                        pe.wait_ge(seeded_r, TS * n + s + 1)
                        pe.wait_ge(hT_ready, TS * n + s + 1)
                        gate_product(r_ps, 0, 0, hT).then_inc(r_done, 1)
                        pe.wait_ge(seeded_zc, TS * n + s + 1)
                        gate_product(zc_ps, 0, 1, hT).then_inc(z_done, 1)
                    if proj and s == XP_STEP - 1:
                        transpose_x1(n)
                    if proj and XP_STEP <= s < Y_STEP:
                        project(n, (s - XP_STEP) // 2, (s - XP_STEP) % 2)
                    if outs and Y_STEP <= s < DN_STEP:
                        output(n, s - Y_STEP)
                    if moe:
                        for d in DN_GAP1.get(s, []):
                            down_shared(n, int(d[1])) if isinstance(d, str) else down(n, d)
                    if scan:
                        pe.wait_ge(rhT_ready, TS * n + s + 1)
                        pe.wait_ge(tz_ready, TS * n + s + 1)
                        gate_product(zc_ps, GW, 2, rhT[:, :].rearrange("p (i q) -> p i q", i=NI)).then_inc(c_done, 1)
                    if moe:
                        u = up_unit(s)
                        if u is not None:
                            up(n, u, 0)
                            up(n, u, 1)
                        for e in DN_GAP2.get(s, []):
                            down(n, e)

            pe.wait_ge(ld_w13, 32)
            pe.wait_ge(ld_we1, 16)
            pe.wait_ge(ld_w2, 16)
            pe.wait_ge(ld_we2, 16)
            iterations(pe, body)


_INS = ['x', 'cond_1024', 'L0_cond_router_W', 'L0_cond_router_bias', 'L0_cond_w1', 'L0_cond_w3', 'L0_cond_w2',
        'L0_cond_W1e', 'L0_cond_W2e', 'L1_cond_Wxz', 'L1_cond_bxz', 'L1_cond_Whz', 'L1_cond_bhz', 'L1_cond_Wxr',
        'L1_cond_bxr', 'L1_cond_Whr', 'L1_cond_bhr', 'L1_cond_Wxh', 'L1_cond_bxh', 'L1_cond_Whh', 'L1_cond_bhh',
        'L1_cond_Whq', 'L1_cond_bhq']


def kernel(**inputs):
    import numpy as np
    import concourse.bacc as bacc
    from concourse.bass_utils import run_bass_kernel_spmd

    nc = bacc.Bacc("TRN2", target_bir_lowering=False, num_devices=1)
    arrays, args = {}, []
    for name in _INS:
        a = np.ascontiguousarray(inputs[name])
        arrays[f"in_{name}"] = a
        args.append(nc.dram_tensor(f"in_{name}", a.shape, mybir.dt.from_np(a.dtype), kind="ExternalInput").ap())
    args.append(nc.dram_tensor("out_0", arrays["in_x"].shape, mybir.dt.float32, kind="ExternalOutput").ap())
    moe_then_gru(nc, *args)
    r = run_bass_kernel_spmd(nc, [arrays], core_ids=[0])
    return r.results[0]["out_0"]
```

```python
import concourse.bass as bass
from concourse import mybir
from contextlib import ExitStack



def moe_then_gru(nc, x, cond, router_w, router_b, w1, w3, w2, we1, we2,
                 wxz, bxz, whz, bhz, wxr, bxr, whr, bhr, wxh, bxh, whh, bhh, whq, bhq, out):
    F32 = mybir.dt.float32
    ALU = mybir.AluOpType
    ACT = mybir.ActivationFunctionType
    AX = mybir.AxisListType

    B, T, C = x.shape
    P = 128
    TS = P // B
    NT = T // TS
    KC = C // P
    HS = w1.shape[1]
    NE = we1.shape[0]
    HE = we1.shape[2]
    NSH = HS // P
    NUP = NSH + NE
    NDN = 1 + NE
    NG = 4
    GW = C // NG
    Q = 32
    NI = GW // Q
    GATES = 3
    RW = GATES * GW
    TOP_K = 2
    HALF = TS // 2

    ctx = ExitStack()
    with ctx:
        def sb(name, shape):
            return ctx.enter_context(nc.sbuf_tensor(name, shape, F32))

        def sem(name):
            return ctx.enter_context(nc.semaphore(name))

        x_all = sb("x_all", [P, NT, C])
        xT_all = sb("xT_all", [P, NT, KC, P])
        cond_tok = sb("cond_tok", [P, C])
        condT = sb("condT", [P, KC, P])
        rw_sb = sb("rw_sb", [P, 2 * KC, NE])
        rbias = sb("rbias", [P, NE])
        w1_sb = sb("w1_sb", [P, KC, HS])
        w3_sb = sb("w3_sb", [P, KC, HS])
        w2_sb = sb("w2_sb", [P, NSH, C])
        we1_sb = sb("we1_sb", [P, NE, KC, HE])
        we2_sb = sb("we2_sb", [P, NE, HE // P, C])
        raw = [sb(f"raw{i}", [P, KC, C]) for i in range(7)]
        ordered = {r: sb(f"ordered{r}", [P, KC, C]) for r in (1, 3, 5, 6)}
        wxT = sb("wxT", [P, KC, NG, GATES, GW])
        whT = sb("whT", [P, GATES, NI, C])
        wqT = sb("wqT", [P, NI, C])
        bias_x = sb("bias_x", [P, NG, GATES, GW])
        bias_h = sb("bias_h", [P, NG, GATES, GW])
        bias_q = sb("bias_q", [P, C])
        ident = sb("ident", [P, P])
        zeros = sb("zeros", [P, P])
        rank = sb("rank", [P, NE])
        logits = sb("logits", [P, NT, NE])
        rbase = sb("rbase", [P, NE])
        score = sb("score", [P, NT, NE])
        sel = sb("sel", [P, NT, NE])
        hit = sb("hit", [P, NT, NE])
        first = sb("first", [P, NT, NE])
        mask = sb("mask", [P, NT, NE])
        gates_all = sb("gates_all", [P, NT, NE])
        best = sb("best", [P, NT])
        den = sb("den", [P, NT])
        rden = sb("rden", [P, NT])
        okay = sb("okay", [P, NT])
        xT_cur = sb("xT_cur", [P, KC, P])
        x_cur = sb("x_cur", [P, C])
        gates_cur = sb("gates_cur", [P, NE])
        sig = sb("sig", [P, NSH, P])
        hid = sb("hid", [P, NUP, 2 * P])
        acc = sb("acc", [P, C])
        x1_cur = sb("x1_cur", [P, C])
        x1T = sb("x1T", [P, KC, P])
        xproj = sb("xproj", [P, NG, RW])
        xs = sb("xs", [P, TS, RW])
        h0_rows = sb("h0_rows", [P, NI, Q])
        t_r = sb("t_r", [P, NI, Q])
        t_z = sb("t_z", [P, NI, Q])
        t_h = sb("t_h", [P, NI, Q])
        t_rT = sb("t_rT", [P, NI, Q])
        t_zT = sb("t_zT", [P, NI, Q])
        t_hT = sb("t_hT", [P, NI, Q])
        rhT = sb("rhT", [P, NI, B])
        zsT = sb("zsT", [P, NI, B])
        candT = sb("candT", [P, NI, B])
        h0T = sb("h0T", [P, NI, Q])
        hist = sb("hist", [P, TS, NI, B])
        yst = sb("yst", [P, NI, P])
        x_res = sb("x_res", [P, C])
        y_bias = sb("y_bias", [P, C])
        y_out = sb("y_out", [P, C])

        bank = [ctx.enter_context(nc.psum_tensor(f"bank{i}", [P, 512], F32)) for i in range(8)]
        r_ps, zc_ps = bank[0], bank[1]
        up_ps = bank[2:5]
        dn_ps = bank[5:7]
        misc = bank[7]
        tr_ps = bank[2:6]

        by_token = nc.dram_tensor("gate_inputs_by_token", [P, NG, RW], F32, kind="Internal").ap()

        ld_x = sem("ld_x")
        ld_router = sem("ld_router")
        ld_gru = sem("ld_gru")
        ld_bias = sem("ld_bias")
        ld_w13 = sem("ld_w13")
        ld_w2 = sem("ld_w2")
        ld_we1 = sem("ld_we1")
        ld_we2 = sem("ld_we2")
        ident0 = sem("ident0")
        ident_ready = sem("ident_ready")
        consts_ready = sem("consts_ready")
        ordered_done = sem("ordered_done")
        tr_done = sem("tr_done")
        tr_act = sem("tr_act")
        tr_dve = sem("tr_dve")
        logits_done = sem("logits_done")
        logits_ready = sem("logits_ready")
        score_ready = sem("score_ready")
        gates_ready = sem("gates_ready")
        dve_setup = sem("dve_setup")
        bias_ready = sem("bias_ready")
        xT_loaded = sem("xT_loaded")
        xg_loaded = sem("xg_loaded")
        up_done = sem("up_done")
        sig_done = sem("sig_done")
        silu_done = sem("silu_done")
        shared_ready = sem("shared_ready")
        gelu_ready = sem("gelu_ready")
        dn_done = sem("dn_done")
        acc_done = sem("acc_done")
        x1_done = sem("x1_done")
        x1_stored = sem("x1_stored")
        x1T_done = sem("x1T_done")
        x1T_ready = sem("x1T_ready")
        xp_done = sem("xp_done")
        xp_ready = sem("xp_ready")
        xp_stored = sem("xp_stored")
        xs_first = sem("xs_first")
        xs_second = sem("xs_second")
        bits_set = sem("bits_set")
        seeded_r = sem("seeded_r")
        seeded_zc = sem("seeded_zc")
        hT_ready = sem("hT_ready")
        r_done = sem("r_done")
        z_done = sem("z_done")
        c_done = sem("c_done")
        tr_ready = sem("tr_ready")
        tz_ready = sem("tz_ready")
        th_ready = sem("th_ready")
        trT_done = sem("trT_done")
        tzT_done = sem("tzT_done")
        thT_done = sem("thT_done")
        rhT_ready = sem("rhT_ready")
        cand_done = sem("cand_done")
        yst_ready = sem("yst_ready")
        y_done = sem("y_done")
        x_res_loaded = sem("x_res_loaded")
        y_bias_done = sem("y_bias_done")
        y_ready = sem("y_ready")
        out_stored = sem("out_stored")

        XG = NT * KC // 4
        WORDER = [(0, "x", 0), (2, "x", 1), (4, "x", 2), (1, "h", 0), (3, "h", 1), (5, "h", 2), (6, "q", 0)]
        WSCALE = {"x": [1.0, 1.0, 1.0], "h": [0.5, 0.5, 0.25], "q": [0.5]}
        WGROUPS = [(r, kind, gate, k) for r, kind, gate in WORDER for k in range(KC)]
        NTR = XG + 1 + len(WGROUPS)
        gru_w = [wxr, whr, wxz, whz, wxh, whh, whq]
        gate_bx = [bxr, bxz, bxh]
        gate_bh = [bhr, bhz, bhh]
        LDX, LDR, LDG = 16 * B, 16 * (2 + B), 16 * (7 + NG)
        LDB = 16 * (2 * GATES * 1 + 1)

        def evacuate(m):
            src = tr_ps[m % 4]
            if m < XG:
                n = 4 // KC
                return xT_all[:, m * n:(m + 1) * n, :, :].rearrange("p n k t -> p (n k t)"), src[:, 0:512], 1.0
            if m == XG:
                return condT[:, :, :].rearrange("p k t -> p (k t)"), src[:, 0:C], 1.0
            _, kind, gate, k = WGROUPS[m - XG - 1]
            s = WSCALE[kind][gate]
            if kind == "x":
                return wxT[:, k, :, gate, :], src[:, 0:C].rearrange("p (j n) -> p j n", j=NG), s
            if kind == "h":
                return whT[:, gate, k, :], src[:, 0:C], s
            return wqT[:, k, :], src[:, 0:C], s

        XP_STEP = 2
        Y_STEP = XP_STEP + KC * GATES
        UP_MM = 2 * KC
        UP_GAP1 = {0: range(0, 2), 1: range(7, 9)}
        UP_GAP2 = {0: range(2, 7), **{s: range(4 + 5 * s, min(9 + 5 * s, NUP * UP_MM)) for s in range(1, 9)}}
        ACT_GAP1 = {1: [0], 2: [2], 3: [3], 4: [4, 5], 5: [6], 6: [7], 7: [8], 8: [9, 10], 9: [11]}
        ACT_GAP2 = {1: [1]}
        SILU_GAP1 = {1: 0, 2: 2, 3: 3}
        SILU_GAP2 = {1: 1}
        DN_GAP1 = {10: [("shared", 2)], 11: [(0, 1)], 12: [(2, 0)], 13: [(3, 1)], 14: [(5, 0)], 15: [(6, 1)]}
        DN_GAP2 = {9: [("shared", 0), ("shared", 1)], 10: [("shared", 3), (0, 0)], 11: [(1, 0), (1, 1)],
                   12: [(2, 1), (3, 0)], 13: [(4, 0), (4, 1)], 14: [(5, 1), (6, 0)], 15: [(7, 0), (7, 1)]}
        ADD_GAP1 = {12: 2, 14: 5}
        ADD_GAP2 = {10: 0, 11: 1, 12: 3, 13: 4, 14: 6, 15: 7}

        def stages(n):
            return 0 <= n < NT, n + 2 < NT, 0 <= n + 1 < NT, 0 <= n - 1 < NT

        def iterations(eng, body):
            for n in (-2, -1, 0, 1):
                body(n, *stages(n), n + 3 < NT)
            with eng.Fori(2, NT - 3) as i:
                body(i, True, True, True, True, True)
            for n in range(NT - 3, NT + 1):
                body(n, *stages(n), n + 3 < NT)

        def above(n, least):
            return n >= least if isinstance(n, int) else True

        block = ctx.enter_context(nc.Block())

        @block.sync
        def _(sp):
            for b in range(B):
                sp.dma_start(x_all[b * TS:(b + 1) * TS, :, :],
                             x[b, :, :].rearrange("(n t) c -> t n c", t=TS)).then_inc(ld_x, 16)
            sp.dma_start(rw_sb[:, :, :], router_w.rearrange("(k p) e -> p k e", p=P)).then_inc(ld_router, 16)
            sp.dma_start(rbias[:, :], router_b.rearrange("(a e) -> a e", a=1).to_broadcast([P, NE])).then_inc(ld_router, 16)
            for b in range(B):
                sp.dma_start(cond_tok[b * TS:(b + 1) * TS, :],
                             cond[b:b + 1, :].to_broadcast([TS, C])).then_inc(ld_router, 16)
            for r in range(7):
                sp.dma_start(raw[r][:, :, :], gru_w[r].rearrange("(o p) c -> p o c", p=P)).then_inc(ld_gru, 16)
            sp.wait_ge(consts_ready, 1)
            for j in range(NG):
                sp.dma_start(h0_rows[Q * j:Q * j + B, :, :], cond[:, GW * j:GW * (j + 1)].rearrange("b (i q) -> b i q", i=NI)).then_inc(ld_gru, 16)
            sp.dma_start(w1_sb[:, :, :], w1.rearrange("(k p) h -> p k h", p=P)).then_inc(ld_w13, 16)
            sp.dma_start(w3_sb[:, :, :], w3.rearrange("(k p) h -> p k h", p=P)).then_inc(ld_w13, 16)
            sp.dma_start(we1_sb[:, :, :, :], we1.rearrange("e (k p) h -> p e k h", p=P)).then_inc(ld_we1, 16)
            sp.dma_start(w2_sb[:, :, :], w2.rearrange("(k p) c -> p k c", p=P)).then_inc(ld_w2, 16)
            sp.dma_start(we2_sb[:, :, :, :], we2.rearrange("e (k p) c -> p e k c", p=P)).then_inc(ld_we2, 16)
            for gate in range(GATES):
                for dst, src in ((bias_x, gate_bx[gate]), (bias_h, gate_bh[gate])):
                    sp.dma_start(dst[:, :, gate, :], src.rearrange("(a j n) -> a j n", a=1, j=NG)
                                 .to_broadcast([P, NG, GW])).then_inc(ld_bias, 16)
            sp.dma_start(bias_q[:, :], bhq.rearrange("(a c) -> a c", a=1).to_broadcast([P, C])).then_inc(ld_bias, 16)
            sp.wait_ge(tr_act, 1)
            sp.dma_start(xT_cur[:, :, :], xT_all[:, 0, :, :]).then_inc(xT_loaded, 16)

            def gate_rows(half, done):
                for j in range(NG):
                    src = by_token[:, j, :].rearrange("(b t) c -> b t c", b=B)[:, half * HALF:(half + 1) * HALF, :]
                    sp.dma_start(xs[Q * j:Q * j + B, half * HALF:(half + 1) * HALF, :], src).then_inc(done, 16)

            def body(n, scan, moe, proj, outs, more):
                if moe:
                    if above(n, -1):
                        sp.wait_ge(x1_done, n + 2)
                    sp.wait_ge(gates_ready, 1)
                    sp.dma_start(x_cur[:, :], x_all[:, bass.ds(n + 2, 1), :].rearrange("p a c -> p (a c)")).then_inc(xg_loaded, 16)
                    sp.dma_start(gates_cur[:, :], gates_all[:, bass.ds(n + 2, 1), :].rearrange("p a c -> p (a c)")).then_inc(xg_loaded, 16)
                if proj:
                    sp.wait_ge(x1_done, n + 2)
                    sp.dma_start(x_all[:, bass.ds(n + 1, 1), :].rearrange("p a c -> p (a c)"), x1_cur[:, :]).then_inc(x1_stored, 16)
                if outs:
                    if above(n, 2):
                        sp.wait_ge(y_ready, n - 1)
                    if not proj:
                        sp.wait_ge(x1_stored, 16 * n)
                    sp.dma_start(x_res[:, :], x_all[:, bass.ds(n - 1, 1), :].rearrange("p a c -> p (a c)")).then_inc(x_res_loaded, 16)
                if proj:
                    sp.wait_ge(xp_ready, GATES * (n + 2))
                    sp.dma_start(by_token, xproj[:, :, :]).then_inc(xp_stored, 16)
                    sp.wait_ge(xp_stored, 16 * (n + 2))
                    gate_rows(0, xs_first)
                if outs:
                    sp.wait_ge(y_ready, n)
                    sp.dma_start(out_tile(n - 1), y_out[:, :]).then_inc(out_stored, 16)
                if more:
                    sp.wait_ge(up_done, NUP * (n + 3))
                    sp.dma_start(xT_cur[:, :, :], xT_all[:, bass.ds(n + 3, 1), :, :].rearrange("p a k t -> p (a k) t")).then_inc(xT_loaded, 16)
                if proj:
                    if scan:
                        sp.wait_ge(seeded_zc, TS * (n + 1))
                    gate_rows(1, xs_second)

            def out_tile(n):
                return out[:, bass.ds(n * TS, TS), :]

            iterations(sp, body)
            sp.wait_ge(out_stored, 16 * NT)

        @block.gpsimd
        def _(pool):
            pool.memset(h0_rows[:, :, :], 0.0).then_inc(ident0, 1)
            pool.memset(ident[:, :], 0.0).then_inc(ident0, 1)
            pool.wait_ge(ident0, 2)
            pool.affine_select(out=ident[:, :], in_=ident[:, :], compare_op=ALU.not_equal, fill=1.0, base=0,
                               pattern=[[-1, P]], channel_multiplier=1).then_inc(ident_ready, 1)
            for e in range(NE):
                pool.memset(rank[:, e:e + 1], float(NE - e)).then_inc(ident0, 1)
            pool.memset(zeros[:, :], 0.0).then_inc(ident0, 1)
            pool.memset(xs[:, :, :], 0.0).then_inc(ident0, 1)
            pool.wait_ge(ident0, 2 + NE + 2)
            pool.drain().then_inc(consts_ready, 1)

            pool.wait_ge(ld_gru, LDG)
            for r, w in ordered.items():
                for o in range(KC):
                    pool.tensor_copy(w[:, o, :].rearrange("p (i j c) -> p i j c", i=NI, j=NG),
                                     raw[r][:, o, :].rearrange("p (j i c) -> p i j c", j=NG, i=NI)).then_inc(ordered_done, 1)

        @block.scalar
        def _(act):
            for m in range(0, NTR, 2):
                act.wait_ge(tr_done, m + 1)
                dst, src, s = evacuate(m)
                act.activation(dst, src, ACT.Copy, scale=s).then_inc(tr_act, 1)
            act.wait_ge(logits_ready, 1)
            act.activation(score[:, :, :], logits[:, :, :], ACT.Sigmoid).then_inc(score_ready, 1)

            def consume_up(n, u):
                ps = up_ps[u % len(up_ps)]
                act.wait_ge(up_done, NUP * (n + 2) + u + 1)
                if u < NSH:
                    act.activation(sig[:, u, :], ps[:, 0:P], ACT.Tanh, scale=0.5).then_inc(sig_done, 1)
                else:
                    act.activation(hid[:, u, :], ps[:, 0:2 * P], ACT.Gelu).then_inc(gelu_ready, 1)

            def seed(n, s, ps, cols, used, done):
                if s == 0:
                    act.wait_ge(xs_first, 16 * NG * (n + 1))
                if s == HALF:
                    act.wait_ge(xs_second, 16 * NG * (n + 1))
                if isinstance(n, int) and n == 0 and s == 0:
                    act.wait_ge(bits_set, 2)
                    act.wait_ge(consts_ready, 1)
                else:
                    act.wait_ge(used, TS * n + s)
                act.activation(ps[:, 0:cols.stop - cols.start], xs[:, s, cols], ACT.Copy).then_inc(done, 1)

            def seed_r(n, s):
                seed(n, s, r_ps, slice(0, GW), tr_ready, seeded_r)

            def seed_zc(n, s):
                seed(n, s, zc_ps, slice(GW, RW), th_ready, seeded_zc)

            def body(n, scan, moe, proj, outs, more):
                for s in range(TS):
                    after = (n, s + 1) if s + 1 < TS and scan else (n + 1, 0) if s + 1 == TS and proj else None
                    if scan:
                        act.wait_ge(r_done, TS * n + s + 1)
                        act.activation(t_r[:, :, :].rearrange("p i q -> p (i q)"), r_ps[:, 0:GW], ACT.Tanh, scale=0.5).then_inc(tr_ready, 1)
                    if after:
                        seed_r(*after)
                    if scan:
                        act.wait_ge(z_done, TS * n + s + 1)
                        act.activation(t_z[:, :, :].rearrange("p i q -> p (i q)"), zc_ps[:, 0:GW], ACT.Tanh, scale=0.5).then_inc(tz_ready, 1)
                    if outs and s == 0:
                        act.wait_ge(hT_ready, NI * (TS * n + 1))
                        if above(n, 2):
                            act.wait_ge(y_done, n - 1)
                        act.activation(yst[:, :, :].rearrange("p i (b t) -> p i b t", b=B),
                                       hist[:, :, :, :].rearrange("p t i b -> p i b t"), ACT.Copy).then_inc(yst_ready, 1)
                    if moe:
                        for u in ACT_GAP1.get(s, []):
                            consume_up(n, u)
                    if scan:
                        act.wait_ge(c_done, TS * n + s + 1)
                        act.activation(t_h[:, :, :].rearrange("p i q -> p (i q)"), zc_ps[:, GW:2 * GW], ACT.Tanh).then_inc(th_ready, 1)
                    if after:
                        seed_zc(*after)
                    if moe:
                        for u in ACT_GAP2.get(s, []):
                            consume_up(n, u)
                    if proj and s == XP_STEP - 1:
                        act.wait_ge(x1T_done, n + 2)
                        act.activation(x1T[:, :, :].rearrange("p k t -> p (k t)"), misc[:, 0:C], ACT.Copy)\
                           .then_inc(x1T_ready, 1)

            iterations(act, body)

        @block.vector
        def _(dve):
            chain = [0]

            def link(ins):
                chain[0] += 1
                ins.then_inc(dve_setup, 1)
                dve.wait_ge(dve_setup, chain[0])

            for m in range(1, NTR, 2):
                dve.wait_ge(tr_done, m + 1)
                dst, src, s = evacuate(m)
                dve.tensor_scalar(dst, src, s, None, ALU.mult).then_inc(tr_dve, 1)

            dve.wait_ge(ld_router, LDR)
            dve.wait_ge(consts_ready, 1)
            dve.wait_ge(logits_done, 1)
            over_tiles = lambda a: a.rearrange("p (a e) -> p a e", a=1).to_broadcast([P, NT, NE])
            over_experts = lambda a: a.rearrange("p (n a) -> p n a", a=1).to_broadcast([P, NT, NE])
            link(dve.tensor_copy(rbase[:, :], misc[:, NT * NE:(NT + 1) * NE]))
            dve.tensor_tensor(logits[:, :, :], misc[:, 0:NT * NE].rearrange("p (n e) -> p n e", e=NE),
                              over_tiles(rbase[:, :]), ALU.add).then_inc(logits_ready, 1)
            dve.wait_ge(score_ready, 1)
            link(dve.tensor_tensor(sel[:, :, :], score[:, :, :], over_tiles(rbias[:, :]), ALU.add))
            for k in range(TOP_K):
                link(dve.tensor_reduce(best[:, :], sel[:, :, :], AX.X, ALU.max))
                link(dve.tensor_tensor(hit[:, :, :], sel[:, :, :], over_experts(best[:, :]), ALU.is_equal))
                link(dve.tensor_tensor(hit[:, :, :], hit[:, :, :], over_tiles(rank[:, :]), ALU.mult))
                link(dve.tensor_reduce(best[:, :], hit[:, :, :], AX.X, ALU.max))
                link(dve.tensor_tensor(first[:, :, :], hit[:, :, :], over_experts(best[:, :]), ALU.is_equal))
                if k == 0:
                    link(dve.tensor_copy(mask[:, :, :], first[:, :, :]))
                    link(dve.scalar_tensor_tensor(sel[:, :, :], first[:, :, :], -1e30, sel[:, :, :], ALU.mult, ALU.add))
                else:
                    link(dve.tensor_tensor(mask[:, :, :], mask[:, :, :], first[:, :, :], ALU.add))
            link(dve.tensor_tensor(score[:, :, :], score[:, :, :], mask[:, :, :], ALU.mult))
            link(dve.tensor_reduce(den[:, :], score[:, :, :], AX.X, ALU.add))
            link(dve.tensor_scalar(okay[:, :], den[:, :], 1e-9, None, ALU.is_gt))
            link(dve.tensor_scalar(rden[:, :], den[:, :], 1e-9, None, ALU.add))
            link(dve.reciprocal(rden[:, :], rden[:, :]))
            link(dve.tensor_tensor(rden[:, :], rden[:, :], okay[:, :], ALU.mult))
            link(dve.tensor_scalar(okay[:, :], okay[:, :], -1.0 / TOP_K, 1.0 / TOP_K, ALU.mult, ALU.add))
            link(dve.tensor_tensor(score[:, :, :], score[:, :, :], over_experts(rden[:, :]), ALU.mult))
            link(dve.tensor_tensor(mask[:, :, :], mask[:, :, :], over_experts(okay[:, :]), ALU.mult))
            dve.tensor_tensor(gates_all[:, :, :], score[:, :, :], mask[:, :, :], ALU.add).then_inc(gates_ready, 1)
            dve.wait_ge(ld_bias, LDB)
            dve.tensor_tensor(bias_x[:, :, :, :], bias_x[:, :, :, :], bias_h[:, :, :, :], ALU.add).then_inc(bias_ready, 1)
            dve.wait_ge(ld_gru, LDG)
            link(dve.transpose(h0T[:, :, :].rearrange("p i q -> p (i q)"), h0_rows[:, :, :].rearrange("p i q -> p (i q)")))
            for i in range(NI):
                dve.tensor_scalar(hist[:, TS - 1, i, :], h0T[:, i, 0:B], 2.0, None, ALU.mult).then_inc(hT_ready, 1)

            def shared_hidden(n, u):
                ps = up_ps[u % len(up_ps)]
                dve.wait_ge(sig_done, NSH * (n + 2) + u + 1)
                dve.scalar_tensor_tensor(hid[:, u, P:2 * P], sig[:, u, :], 1.0, ps[:, 0:P], ALU.add, ALU.mult)\
                   .then_inc(silu_done, 1)
                dve.wait_ge(silu_done, NSH * (n + 2) + u + 1)
                dve.tensor_tensor(hid[:, u, 0:P], hid[:, u, P:2 * P], ps[:, P:2 * P], ALU.mult).then_inc(shared_ready, 1)

            def accumulate(n, g):
                ps = dn_ps[g % 2]
                dve.wait_ge(dn_done, NDN * (n + 2) + g + 1)
                if g == 0:
                    if above(n, -1):
                        dve.wait_ge(x1_done, n + 2)
                    dve.tensor_scalar(acc[:, :], ps[:, 0:C], 0.5, None, ALU.mult).then_inc(acc_done, 1)
                    return
                if g == 1:
                    dve.wait_ge(xg_loaded, 32 * (n + 3))
                dve.wait_ge(acc_done, NDN * (n + 2) + g)
                dve.scalar_tensor_tensor(acc[:, :], ps[:, 0:C], gates_cur[:, g - 1:g], acc[:, :],
                                         ALU.mult, ALU.add).then_inc(acc_done, 1)

            def finish_x1(n):
                dve.wait_ge(acc_done, NDN * (n + 2))
                if above(n, 0):
                    dve.wait_ge(x1T_done, n + 1)
                    dve.wait_ge(x1_stored, 16 * (n + 1))
                dve.scalar_tensor_tensor(x1_cur[:, :], acc[:, :], 1.0 / (1 + TOP_K), x_cur[:, :],
                                         ALU.mult, ALU.add).then_inc(x1_done, 1)

            def add_bias(n, q):
                dve.wait_ge(xp_done, GATES * (n + 1) + q + 1)
                if isinstance(n, int) and n == -1:
                    dve.wait_ge(bias_ready, 1)
                else:
                    dve.wait_ge(xp_stored, 16 * (n + 1))
                    dve.wait_ge(xs_second, 16 * NG * (n + 1))
                    if q == GATES - 1:
                        dve.wait_ge(seeded_zc, TS * n + HALF)
                cols = slice(q * C, (q + 1) * C)
                dve.tensor_tensor(xproj[:, :, :].rearrange("p j c -> p (j c)")[:, cols],
                                  misc[:, 0:C],
                                  bias_x[:, :, :, :].rearrange("p j g c -> p (j g c)")[:, cols],
                                  ALU.add).then_inc(xp_ready, 1)

            def finish_out(n):
                dve.wait_ge(y_done, n)
                if above(n, 2):
                    dve.wait_ge(y_ready, n - 1)
                dve.tensor_tensor(y_bias[:, :], misc[:, 0:C], bias_q[:, :], ALU.add).then_inc(y_bias_done, 1)

            def add_x1(n):
                dve.wait_ge(y_bias_done, n)
                dve.wait_ge(x_res_loaded, 16 * n)
                if above(n, 2):
                    dve.wait_ge(out_stored, 16 * (n - 1))
                dve.tensor_tensor(y_out[:, :], y_bias[:, :], x_res[:, :], ALU.add).then_inc(y_ready, 1)

            def body(n, scan, moe, proj, outs, more):
                for s in range(TS):
                    old, new = hist[:, (s - 1) % TS, :, :], hist[:, s, :, :]
                    g = NI * (TS * n + s)
                    if scan:
                        dve.wait_ge(tr_ready, TS * n + s + 1)
                        for i in range(NI):
                            dve.transpose(t_rT[:, i, :], t_r[:, i, :]).then_inc(trT_done, 1)
                        for i in range(NI):
                            dve.wait_ge(trT_done, g + i + 1)
                            dve.scalar_tensor_tensor(rhT[:, i, :], t_rT[:, i, 0:B], 1.0, old[:, i, :], ALU.add, ALU.mult)\
                               .then_inc(rhT_ready, 1)
                        dve.wait_ge(tz_ready, TS * n + s + 1)
                        dve.transpose(t_zT[:, :, :].rearrange("p i q -> p (i q)"), t_z[:, :, :].rearrange("p i q -> p (i q)"))\
                           .then_inc(tzT_done, 1)
                        dve.wait_ge(tzT_done, TS * n + s + 1)
                        dve.scalar_tensor_tensor(zsT[:, :, :], t_zT[:, :, 0:B], 1.0, old, ALU.add, ALU.mult)
                    if s == 0 and proj:
                        accumulate(n - 1, NDN - 1)
                    if outs and s == Y_STEP + NI:
                        add_x1(n)
                    if moe and s in SILU_GAP1:
                        shared_hidden(n, SILU_GAP1[s])
                    if moe and s in ADD_GAP1:
                        accumulate(n, ADD_GAP1[s])
                    if scan:
                        dve.wait_ge(th_ready, TS * n + s + 1)
                        for i in range(NI):
                            dve.transpose(t_hT[:, i, :], t_h[:, i, :]).then_inc(thT_done, 1)
                        for i in range(NI):
                            dve.wait_ge(thT_done, g + i + 1)
                            dve.scalar_tensor_tensor(candT[:, i, :], t_zT[:, i, 0:B], -1.0, t_hT[:, i, 0:B], ALU.add, ALU.mult)\
                               .then_inc(cand_done, 1)
                        for i in range(NI):
                            dve.wait_ge(cand_done, g + i + 1)
                            dve.scalar_tensor_tensor(new[:, i, :], zsT[:, i, :], 0.5, candT[:, i, :], ALU.mult, ALU.subtract)\
                               .then_inc(hT_ready, 1)
                    if s == 0 and proj:
                        finish_x1(n)
                    if moe and s in SILU_GAP2:
                        shared_hidden(n, SILU_GAP2[s])
                    if proj and s >= XP_STEP and (s - XP_STEP) % 2 == 1 and s < Y_STEP:
                        add_bias(n, (s - XP_STEP) // 2)
                    if outs and s == Y_STEP + NI - 1:
                        finish_out(n)
                    if moe and s in ADD_GAP2:
                        accumulate(n, ADD_GAP2[s])

            iterations(dve, body)

        @block.tensor
        def _(pe):
            pe.wait_ge(ident_ready, 1)
            pe.wait_ge(consts_ready, 1)
            for p in (r_ps, zc_ps):
                pe.matmul(p[:, 0:2 * GW], zeros[:, :], zeros[:, 0:2 * GW], start=True, stop=True).then_inc(bits_set, 1)

            def transposes(m):
                if m >= 4:
                    pe.wait_ge(tr_act if m % 2 == 0 else tr_dve, (m - 4) // 2 + 1)
                dst = tr_ps[m % 4]
                if m < XG:
                    blocks = [x_all[:, (4 * m + i) // KC, ((4 * m + i) % KC) * P:((4 * m + i) % KC + 1) * P] for i in range(4)]
                elif m == XG:
                    blocks = [cond_tok[:, k * P:(k + 1) * P] for k in range(KC)]
                else:
                    r, kind, gate, k = WGROUPS[m - XG - 1]
                    blocks = [(raw[r] if kind == "x" else ordered[r])[:, o, k * P:(k + 1) * P] for o in range(KC)]
                for i, blk in enumerate(blocks):
                    last = pe.transpose(dst[:, i * P:(i + 1) * P], blk, ident[:, :])
                last.then_inc(tr_done, 1)

            pe.wait_ge(ld_x, LDX)
            for m in range(XG):
                transposes(m)
            pe.wait_ge(ld_router, LDR)
            transposes(XG)
            pe.wait_ge(ld_gru, LDG)
            pe.wait_ge(ordered_done, len(ordered) * KC)
            for m in range(XG + 1, NTR):
                transposes(m)
            pe.wait_ge(tr_act, XG // 2 + 1)
            pe.wait_ge(tr_dve, XG // 2)
            for k in range(KC):
                pe.matmul(misc[:, NT * NE:(NT + 1) * NE], condT[:, k, :], rw_sb[:, KC + k, :], start=(k == 0), stop=(k == KC - 1))
            for n in range(NT):
                for k in range(KC):
                    last = pe.matmul(misc[:, n * NE:(n + 1) * NE], xT_all[:, n, k, :], rw_sb[:, k, :],
                                     start=(k == 0), stop=(k == KC - 1))
            last.then_inc(logits_done, 1)
            pe.wait_ge(tr_act, (NTR + 1) // 2)
            pe.wait_ge(tr_dve, NTR // 2)

            def up(n, m):
                u, half, k = m // UP_MM, m % UP_MM // KC, m % KC
                ring = len(up_ps)
                if m % UP_MM == 0:
                    if u == 0:
                        pe.wait_ge(xT_loaded, 16 * (n + 3))
                    if u < ring:
                        if above(n, -1):
                            pe.wait_ge(gelu_ready, NE * (n + 2) + u + 1 - ring)
                    elif u - ring < NSH:
                        pe.wait_ge(shared_ready, NSH * (n + 2) + u + 1 - ring)
                    else:
                        pe.wait_ge(gelu_ready, NE * (n + 2) + u + 1 - ring - NSH)
                if u < NSH:
                    w = (w1_sb, w3_sb)[half][:, k, u * P:(u + 1) * P]
                else:
                    w = we1_sb[:, u - NSH, k, half * P:(half + 1) * P]
                last = pe.matmul(up_ps[u % ring][:, half * P:(half + 1) * P], w, xT_cur[:, k, :],
                                 start=(k == 0), stop=(k == KC - 1))
                if m % UP_MM == UP_MM - 1:
                    last.then_inc(up_done, 1)

            def down_shared(n, u):
                if u == 0:
                    if above(n, -1):
                        pe.wait_ge(acc_done, NDN * (n + 2))
                pe.wait_ge(shared_ready, NSH * (n + 2) + u + 1)
                last = pe.matmul(dn_ps[0][:, 0:C], hid[:, u, 0:P], w2_sb[:, u, :], start=(u == 0), stop=(u == NSH - 1))
                if u == NSH - 1:
                    last.then_inc(dn_done, 1)

            def down(n, e, k):
                if k == 0:
                    pe.wait_ge(gelu_ready, NE * (n + 2) + e + 1)
                    if e > 0:
                        pe.wait_ge(acc_done, NDN * (n + 2) + e)
                last = pe.matmul(dn_ps[(1 + e) % 2][:, 0:C], hid[:, NSH + e, k * P:(k + 1) * P], we2_sb[:, e, k, :],
                                 start=(k == 0), stop=(k == HE // P - 1))
                if k == HE // P - 1:
                    last.then_inc(dn_done, 1)

            def transpose_x1(n):
                pe.wait_ge(x1_done, n + 2)
                if above(n, 2):
                    pe.wait_ge(y_bias_done, n - 1)
                elif above(n, 0):
                    pe.wait_ge(xp_ready, GATES * (n + 1))
                else:
                    pe.wait_ge(logits_ready, 1)
                for k in range(KC):
                    last = pe.transpose(misc[:, k * P:(k + 1) * P], x1_cur[:, k * P:(k + 1) * P], ident[:, :])
                last.then_inc(x1T_done, 1)

            def project(n, q, k):
                if k == 0:
                    if q == 0:
                        pe.wait_ge(x1T_ready, n + 2)
                    if q > 0 or above(n, 0):
                        pe.wait_ge(xp_ready, GATES * (n + 1) + q)
                last = pe.matmul(misc[:, 0:C], x1T[:, k, :],
                                 wxT[:, k, :, :, :].rearrange("p j g c -> p (j g c)")[:, q * C:(q + 1) * C],
                                 start=(k == 0), stop=(k == KC - 1))
                if k == KC - 1:
                    last.then_inc(xp_done, 1)

            def output(n, i, proj):
                if i == 0:
                    pe.wait_ge(yst_ready, n)
                    if proj:
                        pe.wait_ge(xp_ready, GATES * (n + 2))
                    else:
                        pe.wait_ge(y_bias_done, n - 1)
                last = pe.matmul(misc[:, 0:C], yst[:, i, :], wqT[:, i, :], start=(i == 0), stop=(i == NI - 1))
                if i == NI - 1:
                    last.then_inc(y_done, 1)

            def gate_product(ps, col, gate, lhsT, i):
                for j in range(NG):
                    last = pe.matmul(ps[Q * j:Q * j + B, col:col + GW], lhsT[:, i, :],
                                     whT[:, gate, i, j * GW:(j + 1) * GW], start=False, stop=(i == NI - 1),
                                     tile_position=(0, Q * j), skip_group_check=True)
                return last

            def body(n, scan, moe, proj, outs, more):
                for s in range(TS):
                    hT = hist[:, (s - 1) % TS, :, :]
                    g = NI * (TS * n + s)
                    if scan:
                        for i in range(NI):
                            pe.wait_ge(hT_ready, g + i + 1)
                            if i == 0:
                                pe.wait_ge(seeded_r, TS * n + s + 1)
                            last = gate_product(r_ps, 0, 0, hT, i)
                        last.then_inc(r_done, 1)
                        pe.wait_ge(seeded_zc, TS * n + s + 1)
                        for i in range(NI):
                            last = gate_product(zc_ps, 0, 1, hT, i)
                        last.then_inc(z_done, 1)
                    if proj and s == XP_STEP - 1:
                        transpose_x1(n)
                    if proj and XP_STEP <= s < Y_STEP:
                        project(n, (s - XP_STEP) // 2, (s - XP_STEP) % 2)
                    if outs and Y_STEP <= s < Y_STEP + NI:
                        output(n, s - Y_STEP, proj)
                    if moe:
                        for m in UP_GAP1.get(s, []):
                            up(n, m)
                        for e, k in DN_GAP1.get(s, []):
                            down_shared(n, k) if e == "shared" else down(n, e, k)
                    if scan:
                        for i in range(NI):
                            pe.wait_ge(rhT_ready, g + i + 1)
                            if i == 0:
                                pe.wait_ge(tz_ready, TS * n + s + 1)
                            last = gate_product(zc_ps, GW, 2, rhT, i)
                        last.then_inc(c_done, 1)
                    if moe:
                        for m in UP_GAP2.get(s, []):
                            up(n, m)
                        for e, k in DN_GAP2.get(s, []):
                            down_shared(n, k) if e == "shared" else down(n, e, k)

            pe.wait_ge(ld_w13, 32)
            pe.wait_ge(ld_we1, 16)
            pe.wait_ge(ld_w2, 16)
            pe.wait_ge(ld_we2, 16)
            iterations(pe, body)


_INS = ['x', 'cond_1024', 'L0_cond_router_W', 'L0_cond_router_bias', 'L0_cond_w1', 'L0_cond_w3', 'L0_cond_w2',
        'L0_cond_W1e', 'L0_cond_W2e', 'L1_cond_Wxz', 'L1_cond_bxz', 'L1_cond_Whz', 'L1_cond_bhz', 'L1_cond_Wxr',
        'L1_cond_bxr', 'L1_cond_Whr', 'L1_cond_bhr', 'L1_cond_Wxh', 'L1_cond_bxh', 'L1_cond_Whh', 'L1_cond_bhh',
        'L1_cond_Whq', 'L1_cond_bhq']


def kernel(**inputs):
    import numpy as np
    import concourse.bacc as bacc
    from concourse.bass_utils import run_bass_kernel_spmd

    nc = bacc.Bacc("TRN2", target_bir_lowering=False, num_devices=1)
    arrays, args = {}, []
    for name in _INS:
        a = np.ascontiguousarray(inputs[name])
        arrays[f"in_{name}"] = a
        args.append(nc.dram_tensor(f"in_{name}", a.shape, mybir.dt.from_np(a.dtype), kind="ExternalInput").ap())
    args.append(nc.dram_tensor("out_0", arrays["in_x"].shape, mybir.dt.float32, kind="ExternalOutput").ap())
    moe_then_gru(nc, *args)
    r = run_bass_kernel_spmd(nc, [arrays], core_ids=[0])
    return r.results[0]["out_0"]
```

```python
import concourse.bass as bass
from concourse import mybir
from contextlib import ExitStack



def moe_then_gru(nc, x, cond, router_w, router_b, w1, w3, w2, we1, we2,
                 wxz, bxz, whz, bhz, wxr, bxr, whr, bhr, wxh, bxh, whh, bhh, whq, bhq, out):
    F32 = mybir.dt.float32
    F32R = mybir.dt.float32r
    ALU = mybir.AluOpType
    ACT = mybir.ActivationFunctionType
    AX = mybir.AxisListType

    B, T, C = x.shape
    P = 128
    TS = P // B
    NT = T // TS
    KC = C // P
    HS = w1.shape[1]
    NE = we1.shape[0]
    HE = we1.shape[2]
    NSH = HS // P
    NUP = NSH + NE
    NDN = 1 + NE
    HRING = NE // 2
    NG = 4
    GW = C // NG
    Q = 32
    NI = GW // Q
    GATES = 3
    RW = GATES * GW
    TOP_K = 2
    SHARE = 1.0 / (1 + TOP_K)
    HALF = TS // 2

    ctx = ExitStack()
    with ctx:
        def sb(name, shape, dtype=F32):
            return ctx.enter_context(nc.sbuf_tensor(name, shape, dtype))

        def sem(name):
            return ctx.enter_context(nc.semaphore(name))

        x_all = sb("x_all", [P, NT, C])
        xT_all = sb("xT_all", [P, NT, KC, P])
        cond_tok = sb("cond_tok", [P, C])
        condT = sb("condT", [P, KC, P])
        rw_sb = sb("rw_sb", [P, 2 * KC, NE])
        rw_wide = sb("rw_wide", [P, KC, Q])
        rbias = sb("rbias", [P, NE])
        w1_sb = sb("w1_sb", [P, KC, HS])
        w3_sb = sb("w3_sb", [P, KC, HS])
        w2_sb = sb("w2_sb", [P, NSH, C])
        we1_sb = sb("we1_sb", [P, NE, KC, HE])
        gru_raw = sb("gru_raw", [P, 11, KC, C])
        raw = [gru_raw[:, r, :, :] for r in range(7)]
        ordered = {r: gru_raw[:, 7 + i, :, :] for i, r in enumerate((1, 3, 5, 6))}
        we2_raw = gru_raw[:, 0:NE, :, :]
        we2_high = sb("we2_high", [P, NE, HE // P, C], F32R)
        we2_low = sb("we2_low", [P, NE, HE // P, C], F32R)
        wxT = sb("wxT", [P, KC, NG, GATES, GW])
        whT = sb("whT", [P, GATES, NI, C])
        wqT = sb("wqT", [P, NI, C])
        bias_x = sb("bias_x", [P, NG, GATES, GW])
        bias_h = sb("bias_h", [P, NG, GATES, GW])
        bias_q = sb("bias_q", [P, C])
        ident = sb("ident", [P, P])
        zeros = sb("zeros", [P, P])
        rank = sb("rank", [P, NE])
        logits = sb("logits", [P, NT, NE])
        rbase = sb("rbase", [P, NE])
        score = sb("score", [P, NT, NE])
        sel = sb("sel", [P, NT, NE])
        hit = sb("hit", [P, NT, NE])
        first = sb("first", [P, NT, NE])
        mask = sb("mask", [P, NT, NE])
        gates_all = sb("gates_all", [P, NT, NE])
        best = sb("best", [P, NT])
        den = sb("den", [P, NT])
        rden = sb("rden", [P, NT])
        okay = sb("okay", [P, NT])
        xT_cur = sb("xT_cur", [P, KC, P])
        x_cur = sb("x_cur", [P, C])
        gates_cur = sb("gates_cur", [P, NE])
        sig = sb("sig", [P, NSH, P])
        hid = sb("hid", [P, NSH, P])
        hid_full = sb("hid_full", [P, 2, 2 * P])
        hid_high = sb("hid_high", [P, HRING, 2 * P], F32R)
        hid_low = sb("hid_low", [P, HRING, 2 * P], F32R)
        acc = sb("acc", [P, C])
        x1_cur = sb("x1_cur", [P, C])
        x1T = sb("x1T", [P, KC, P])
        spent = gru_raw[:, :, :, :].rearrange("p r o c -> p (r o c)")
        xs = spent[:, 0:TS * RW].rearrange("p (t c) -> p t c", t=TS)
        spent = spent[:, TS * RW:]
        xproj = spent[:, 0:NG * RW].rearrange("p (j c) -> p j c", j=NG)
        spent = spent[:, NG * RW:]
        x_res, y_bias, y_out = (spent[:, i * C:(i + 1) * C] for i in range(3))
        yst = spent[:, 3 * C:3 * C + NI * P].rearrange("p (i t) -> p i t", i=NI)
        h0_rows = sb("h0_rows", [P, NI, Q])
        t_r = sb("t_r", [P, NI, Q])
        t_z = sb("t_z", [P, NI, Q])
        t_h = sb("t_h", [P, NI, Q])
        t_rT = sb("t_rT", [P, NI, Q])
        t_zT = sb("t_zT", [P, NI, Q])
        rhT = sb("rhT", [P, NI, B])
        h0T = sb("h0T", [P, NI, Q])
        factors = sb("factors", [P, NI, B, 2])
        terms = sb("terms", [P, NI, Q, 2])
        hist = sb("hist", [P, TS, NI, B, 2])

        bank = [ctx.enter_context(nc.psum_tensor(f"bank{i}", [P, 512], F32)) for i in range(8)]
        r_ps, zc_ps = bank[0], bank[1]
        up_ps = bank[2:5]
        dn_ps = bank[5:7]
        misc = bank[7]
        tr_ps = bank[0:4]
        lg_ps = bank[4:6]

        by_token = nc.dram_tensor("gate_inputs_by_token", [P, NG, RW], F32, kind="Internal").ap()

        ld_x = [sem(f"ld_x{h}") for h in range(2)]
        ld_router = sem("ld_router")
        ld_gru = sem("ld_gru")
        ld_bias = sem("ld_bias")
        ld_w13 = sem("ld_w13")
        ld_w2 = sem("ld_w2")
        ld_we1 = sem("ld_we1")
        ld_we2 = [sem(f"ld_we2_{part}") for part in range(3)]
        pool_set = sem("pool_set")
        ident_ready = sem("ident_ready")
        consts_ready = sem("consts_ready")
        ordered_done = sem("ordered_done")
        tr_done = sem("tr_done")
        tr_act = sem("tr_act")
        tr_dve = sem("tr_dve")
        rw_zeroed = sem("rw_zeroed")
        rw_ready = sem("rw_ready")
        lg_done = sem("lg_done")
        lgT_ready = sem("lgT_ready")
        logits_done = sem("logits_done")
        logits_ready = sem("logits_ready")
        score_ready = sem("score_ready")
        gates_ready = sem("gates_ready")
        dve_setup = sem("dve_setup")
        bias_ready = sem("bias_ready")
        xT_loaded = sem("xT_loaded")
        xg_loaded = sem("xg_loaded")
        up_done = sem("up_done")
        sig_done = sem("sig_done")
        silu_done = sem("silu_done")
        shared_ready = sem("shared_ready")
        gelu_ready = sem("gelu_ready")
        dn_done = sem("dn_done")
        acc_done = sem("acc_done")
        x1_stored = sem("x1_stored")
        x1T_done = sem("x1T_done")
        x1T_ready = sem("x1T_ready")
        xp_done = sem("xp_done")
        xp_ready = sem("xp_ready")
        xp_stored = sem("xp_stored")
        xs_first = sem("xs_first")
        xs_second = sem("xs_second")
        bits_set = sem("bits_set")
        we2_high_ready = sem("we2_high_ready")
        we2_split = sem("we2_split")
        xs_zeroed = sem("xs_zeroed")
        low_ready = sem("low_ready")
        seeded_r = sem("seeded_r")
        seeded_zc = sem("seeded_zc")
        hT_ready = sem("hT_ready")
        r_done = sem("r_done")
        z_done = sem("z_done")
        c_done = sem("c_done")
        tr_ready = sem("tr_ready")
        tz_ready = sem("tz_ready")
        th_ready = sem("th_ready")
        trT_done = sem("trT_done")
        tzT_done = sem("tzT_done")
        a_ready = sem("a_ready")
        thT_done = sem("thT_done")
        rhT_ready = sem("rhT_ready")
        yst_ready = sem("yst_ready")
        y_done = sem("y_done")
        kept_busy = sem("kept_busy")
        x_res_loaded = sem("x_res_loaded")
        y_bias_done = sem("y_bias_done")
        y_ready = sem("y_ready")
        out_stored = sem("out_stored")

        XG = NT * KC // 4
        TG = NT // (2 * NG)
        WORDER = [(0, "x", 0), (2, "x", 1), (4, "x", 2), (1, "h", 0), (3, "h", 1), (5, "h", 2), (6, "q", 0)]
        WSCALE = {"x": [1.0, 1.0, 1.0], "h": [1.0, 1.0, 0.5], "q": [1.0]}
        WGROUPS = [(r, kind, gate, k) for r, kind, gate in WORDER for k in range(KC)]
        NTR = XG + 1 + len(WGROUPS)
        LG_AFTER = XG + GATES * KC
        gru_w = [wxr, whr, wxz, whz, wxh, whh, whq]
        gate_bx = [bxr, bxz, bxh]
        gate_bh = [bhr, bhz, bhh]
        LDX, LDR, LDG = 16 * B, 16 * (2 + B), 16 * (len(gru_w) + NG)
        LDB = 16 * (2 * GATES + 1)

        def evacuate(m):
            src = tr_ps[m % 4]
            if m < XG:
                n = 4 // KC
                return xT_all[:, m * n:(m + 1) * n, :, :].rearrange("p n k t -> p (n k t)"), src[:, 0:512], 1.0
            if m == XG:
                return condT[:, :, :].rearrange("p k t -> p (k t)"), src[:, 0:C], 1.0
            _, kind, gate, k = WGROUPS[m - XG - 1]
            s = WSCALE[kind][gate]
            if kind == "x":
                return wxT[:, k, :, gate, :], src[:, 0:C].rearrange("p (j n) -> p j n", j=NG), s
            if kind == "h":
                return whT[:, gate, k, :], src[:, 0:C], s
            return wqT[:, k, :], src[:, 0:C], s

        lgT = [a[:, :, :].rearrange("p u t -> p (u t)") for a in (hid, hid_full)]

        XP_STEP = 2
        Y_STEP = XP_STEP + KC * GATES
        OUT_STEP = 12
        UNITS = [~0, 0, ~1, 1, ~2, 2, ~3, 3] + list(range(NSH, NE))
        UP_MM = 2 * KC
        UP_COUNT1 = [1, 1, 0, 0, 0, 0, 0, 0, 0, 0, 0, 0, 0, 0, 1, 0]
        UP_COUNT2 = [4, 4, 4, 4, 3, 2, 2, 2, 2, 2, 2, 4, 4, 4, 2, 0]
        SHARED = NE
        GROUPS = [0, 1, 2, SHARED] + list(range(3, NE))
        HB = HE // P
        PARTS = [(k, part) for k in range(HB) for part in ("high high", "high low")] + [(k, "low high") for k in range(HB)]
        DN_MM = [(g, k, part) for g, e in enumerate(GROUPS)
                 for k, part in ([(k, "whole") for k in range(NSH)] if e == SHARED else PARTS)]
        DN_COUNT1 = [0, 0, 0, 0, 0, 0, 0, 0, 0, 0, 1, 1, 5, 5, 2, 4]
        DN_COUNT2 = [0, 0, 0, 0, 2, 4, 4, 4, 4, 1, 1, 0, 0, 0, 4, 8]

        def plan(counts1, counts2):
            gap1, gap2, placed = [], [], 0
            for count1, count2 in zip(counts1, counts2):
                gap1.append(range(placed, placed + count1))
                gap2.append(range(placed + count1, placed + count1 + count2))
                placed += count1 + count2
            return gap1, gap2, placed

        UP_GAP1, UP_GAP2, placed = plan(UP_COUNT1, UP_COUNT2)
        assert placed == NUP * UP_MM
        DN_GAP1, DN_GAP2, placed = plan(DN_COUNT1, DN_COUNT2)
        DN_REST = range(placed, len(DN_MM))
        ACT_GAP1 = {2: [1], 4: [3], 7: [5], 11: [7], 12: [8], 13: [9], 14: [10]}
        ACT_GAP2 = {0: [0], 2: [2], 4: [4], 8: [6], 14: [11]}
        SILU_GAP1 = {1: [(0, 0)], 3: [(1, 0)], 5: [(2, 0)], 9: [(3, 0)]}
        SILU_GAP2 = {1: [(0, 1)], 3: [(1, 1)], 5: [(2, 1)], 9: [(3, 1)]}
        LOW_GAP1 = {15: 7}
        LOW_GAP2 = {2: 0, 4: 1, 7: 2, 11: 3, 12: 4, 13: 5, 14: 6}
        ADD_GAP2 = {6: 0, 8: 1, 10: 2, 11: 3, 13: 4, 14: 5, 15: 6}
        WE2_PARTS = [slice(0, 3), slice(3, 7), slice(7, NE)]
        EARLY = 4
        SPLIT_STEP = 3

        def stages(n):
            return 0 <= n < NT, n + 2 < NT, 0 <= n + 1 < NT, 0 <= n - 1 < NT

        def iterations(eng, body):
            for n in (-2, -1, 0, 1):
                body(n, *stages(n), n + 3 < NT)
            with eng.Fori(2, NT - 3) as i:
                body(i, True, True, True, True, True)
            for n in range(NT - 3, NT + 1):
                body(n, *stages(n), n + 3 < NT)

        def dn_bank(g):
            return misc if g == NDN - 1 else dn_ps[g % 2]

        def above(n, least):
            return n >= least if isinstance(n, int) else True

        block = ctx.enter_context(nc.Block())

        @block.sync
        def _(sp):
            for h in range(2):
                for b in range(B):
                    sp.dma_start(x_all[b * TS:(b + 1) * TS, h * NT // 2:(h + 1) * NT // 2, :],
                                 x[b, h * T // 2:(h + 1) * T // 2, :].rearrange("(n t) c -> t n c", t=TS)).then_inc(ld_x[h], 16)
            sp.dma_start(rw_sb[:, :, :], router_w.rearrange("(k p) e -> p k e", p=P)).then_inc(ld_router, 16)
            sp.dma_start(rbias[:, :], router_b.rearrange("(a e) -> a e", a=1).to_broadcast([P, NE])).then_inc(ld_router, 16)
            for b in range(B):
                sp.dma_start(cond_tok[b * TS:(b + 1) * TS, :],
                             cond[b:b + 1, :].to_broadcast([TS, C])).then_inc(ld_router, 16)
            for r in range(7):
                sp.dma_start(raw[r][:, :, :], gru_w[r].rearrange("(o p) c -> p o c", p=P)).then_inc(ld_gru, 16)
            sp.wait_ge(consts_ready, 1)
            for j in range(NG):
                sp.dma_start(h0_rows[Q * j:Q * j + B, :, :], cond[:, GW * j:GW * (j + 1)].rearrange("b (i q) -> b i q", i=NI)).then_inc(ld_gru, 16)
            sp.wait_ge(tr_act, 1)
            sp.dma_start(xT_cur[:, :, :], xT_all[:, 0, :, :]).then_inc(xT_loaded, 16)
            sp.dma_start(w1_sb[:, :, :], w1.rearrange("(k p) h -> p k h", p=P)).then_inc(ld_w13, 16)
            sp.dma_start(w3_sb[:, :, :], w3.rearrange("(k p) h -> p k h", p=P)).then_inc(ld_w13, 16)
            sp.dma_start(we1_sb[:, :, :, :], we1.rearrange("e (k p) h -> p e k h", p=P)).then_inc(ld_we1, 16)
            sp.wait_ge(ordered_done, len(ordered) * KC)
            sp.wait_ge(tr_done, LG_AFTER + 1)
            for part, experts in enumerate(WE2_PARTS):
                if experts.stop > len(raw):
                    sp.wait_ge(tr_done, NTR)
                sp.dma_start(we2_raw[:, experts, :, :], we2[experts].rearrange("e (k p) c -> p e k c", p=P)).then_inc(ld_we2[part], 16)
            for gate in range(GATES):
                for dst, src in ((bias_x, gate_bx[gate]), (bias_h, gate_bh[gate])):
                    sp.dma_start(dst[:, :, gate, :], src.rearrange("(a j n) -> a j n", a=1, j=NG)
                                 .to_broadcast([P, NG, GW])).then_inc(ld_bias, 16)
            sp.dma_start(bias_q[:, :], bhq.rearrange("(a c) -> a c", a=1).to_broadcast([P, C])).then_inc(ld_bias, 16)
            sp.dma_start(w2_sb[:, :, :], w2.rearrange("(k p) c -> p k c", p=P)).then_inc(ld_w2, 16)

            def gate_rows(half, done):
                for j in range(NG):
                    src = by_token[:, j, :].rearrange("(b t) c -> b t c", b=B)[:, half * HALF:(half + 1) * HALF, :]
                    sp.dma_start(xs[Q * j:Q * j + B, half * HALF:(half + 1) * HALF, :], src).then_inc(done, 16)

            def body(n, scan, moe, proj, outs, more):
                if moe:
                    if above(n, -1):
                        sp.wait_ge(acc_done, NDN * (n + 2))
                    sp.dma_start(x_cur[:, :], x_all[:, bass.ds(n + 2, 1), :].rearrange("p a c -> p (a c)")).then_inc(xg_loaded, 16)
                    sp.wait_ge(gates_ready, 2 if above(n, EARLY - 2) else 1)
                    sp.dma_start(gates_cur[:, :], gates_all[:, bass.ds(n + 2, 1), :].rearrange("p a c -> p (a c)")).then_inc(xg_loaded, 16)
                if proj:
                    sp.wait_ge(acc_done, NDN * (n + 2))
                    sp.dma_start(x_all[:, bass.ds(n + 1, 1), :].rearrange("p a c -> p (a c)"), x1_cur[:, :]).then_inc(x1_stored, 16)
                if outs:
                    if above(n, 2):
                        sp.wait_ge(y_ready, n - 1)
                    if not proj:
                        sp.wait_ge(x1_stored, 16 * n)
                    sp.dma_start(x_res[:, :], x_all[:, bass.ds(n - 1, 1), :].rearrange("p a c -> p (a c)")).then_inc(x_res_loaded, 16)
                if proj:
                    sp.wait_ge(xp_ready, GATES * (n + 2))
                    sp.dma_start(by_token, xproj[:, :, :]).then_inc(xp_stored, 16)
                    sp.wait_ge(xp_stored, 16 * (n + 2))
                    if isinstance(n, int) and n == -1:
                        sp.wait_ge(xs_zeroed, 1)
                    gate_rows(0, xs_first)
                if outs:
                    sp.wait_ge(y_ready, n)
                    sp.dma_start(out_tile(n - 1), y_out[:, :]).then_inc(out_stored, 16)
                if more:
                    sp.wait_ge(up_done, NUP * (n + 3))
                    sp.dma_start(xT_cur[:, :, :], xT_all[:, bass.ds(n + 3, 1), :, :].rearrange("p a k t -> p (a k) t")).then_inc(xT_loaded, 16)
                if proj:
                    if scan:
                        sp.wait_ge(seeded_zc, TS * (n + 1))
                    gate_rows(1, xs_second)

            def out_tile(n):
                return out[:, bass.ds(n * TS, TS), :]

            iterations(sp, body)
            sp.wait_ge(out_stored, 16 * NT)

        @block.gpsimd
        def _(pool):
            pool.memset(h0_rows[:, :, :], 0.0).then_inc(pool_set, 1)
            pool.memset(ident[:, :], 0.0).then_inc(pool_set, 1)
            pool.wait_ge(pool_set, 2)
            pool.affine_select(out=ident[:, :], in_=ident[:, :], compare_op=ALU.not_equal, fill=1.0, base=0,
                               pattern=[[-1, P]], channel_multiplier=1).then_inc(ident_ready, 1)
            for e in range(NE):
                pool.memset(rank[:, e:e + 1], float(NE - e)).then_inc(pool_set, 1)
            pool.memset(zeros[:, :], 0.0).then_inc(pool_set, 1)
            pool.memset(factors[:, :, :, :], 0.0).then_inc(pool_set, 1)
            pool.wait_ge(pool_set, 2 + NE + 2)
            pool.drain().then_inc(consts_ready, 1)

            pool.wait_ge(ld_gru, LDG)
            for r, w in ordered.items():
                for o in range(KC):
                    pool.tensor_copy(w[:, o, :].rearrange("p (i j c) -> p i j c", i=NI, j=NG),
                                     raw[r][:, o, :].rearrange("p (j i c) -> p i j c", j=NG, i=NI)).then_inc(ordered_done, 1)
            pool.wait_ge(we2_split, NE)
            pool.memset(xs, 0.0).then_inc(xs_zeroed, 1)

        @block.scalar
        def _(act):
            for m in range(0, NTR, 2):
                act.wait_ge(tr_done, m + 1)
                dst, src, s = evacuate(m)
                act.activation(dst, src, ACT.Copy, scale=s).then_inc(tr_act, 1)
                if m == XG:
                    act.wait_ge(lg_done, 1)
                    act.activation(lgT[0], lg_ps[0][:, :], ACT.Copy).then_inc(lgT_ready, 1)
                if m == LG_AFTER:
                    act.wait_ge(logits_ready, 1)
                    act.activation(score[:, :, :], logits[:, :, :], ACT.Sigmoid).then_inc(score_ready, 1)

            def consume_up(n, place):
                u, ps = UNITS[place], up_ps[place % len(up_ps)]
                act.wait_ge(up_done, NUP * (n + 2) + place + 1)
                if u < 0:
                    act.activation(sig[:, ~u, :], ps[:, 0:P], ACT.Tanh, scale=0.5).then_inc(sig_done, 1)
                else:
                    if u >= 2 or above(n, -1):
                        act.wait_ge(low_ready, NE * (n + 2) + u - 1)
                    act.activation(hid_full[:, u % 2, :], ps[:, 0:2 * P], ACT.Gelu)
                    act.activation(hid_high[:, u % HRING, :], ps[:, 0:2 * P], ACT.Gelu).then_inc(gelu_ready, 1)

            def seed(n, s, ps, cols, used, done):
                if isinstance(n, int) and n == 0 and s == 0:
                    act.wait_ge(bits_set, 2)
                else:
                    act.wait_ge(used, NI * (TS * n + s))
                act.activation(ps[:, 0:cols.stop - cols.start], xs[:, s, cols], ACT.Copy).then_inc(done, 1)

            def seed_r(n, s):
                seed(n, s, r_ps, slice(0, GW), tr_ready, seeded_r)

            def seed_zc(n, s):
                seed(n, s, zc_ps, slice(GW, RW), th_ready, seeded_zc)

            def body(n, scan, moe, proj, outs, more):
                for s in range(TS):
                    after = (n, s + 1) if s + 1 < TS and scan else (n + 1, 0) if s + 1 == TS and proj else None
                    if scan:
                        act.wait_ge(r_done, TS * n + s + 1)
                        for i in range(NI):
                            act.activation(t_r[:, i, :], r_ps[:, i * Q:(i + 1) * Q], ACT.Tanh, scale=0.5).then_inc(tr_ready, 1)
                        act.wait_ge(z_done, TS * n + s + 1)
                        act.activation(t_z[:, :, :].rearrange("p i q -> p (i q)"), zc_ps[:, 0:GW], ACT.Tanh, scale=0.5).then_inc(tz_ready, 1)
                    if after:
                        seed_r(*after)
                    if outs and s == 0:
                        act.wait_ge(hT_ready, NI * (TS * n + 1))
                        if above(n, 2):
                            act.wait_ge(y_done, n - 1)
                        act.activation(yst[:, :, :].rearrange("p i (b t) -> p i b t", b=B),
                                       hist[:, :, :, :, 1].rearrange("p t i b -> p i b t"), ACT.Copy).then_inc(yst_ready, 1)
                    if moe:
                        for u in ACT_GAP1.get(s, []):
                            consume_up(n, u)
                    if scan:
                        act.wait_ge(c_done, TS * n + s + 1)
                        for i in range(NI):
                            act.activation(t_h[:, i, :], zc_ps[:, GW + i * Q:GW + (i + 1) * Q], ACT.Tanh, scale=-1.0).then_inc(th_ready, 1)
                    if scan and s == HALF - 2:
                        act.wait_ge(xs_second, 16 * NG * (n + 1))
                    if proj and s == TS - 2:
                        act.wait_ge(xs_first, 16 * NG * (n + 2))
                    if after:
                        seed_zc(*after)
                    if moe:
                        for u in ACT_GAP2.get(s, []):
                            consume_up(n, u)
                    if isinstance(n, int) and n == -2 and 0 <= s - SPLIT_STEP < NE:
                        e = s - SPLIT_STEP
                        for part, experts in enumerate(WE2_PARTS):
                            if e == experts.start:
                                act.wait_ge(ld_we2[part], 16)
                        act.activation(we2_high[:, e, :, :], we2_raw[:, e, :, :], ACT.Copy).then_inc(we2_high_ready, 1)
                    if proj and s == XP_STEP - 1:
                        act.wait_ge(x1T_done, n + 2)
                        act.activation(x1T[:, :, :].rearrange("p k t -> p (k t)"), misc[:, 0:C], ACT.Copy)\
                           .then_inc(x1T_ready, 1)

            iterations(act, body)

        @block.vector
        def _(dve):
            chain = [0]

            def link(ins):
                chain[0] += 1
                ins.then_inc(dve_setup, 1)
                dve.wait_ge(dve_setup, chain[0])

            dve.memset(rw_wide[:, :, :], 0.0).then_inc(rw_zeroed, 1)

            def over_tiles(a, tiles):
                return a.rearrange("p (a e) -> p a e", a=1).to_broadcast([P, tiles.stop - tiles.start, NE])

            def over_experts(a):
                return a.rearrange("p (n a) -> p n a", a=1).to_broadcast([P, a.shape[-1], NE])

            for m in range(1, NTR, 2):
                dve.wait_ge(tr_done, m + 1)
                dst, src, s = evacuate(m)
                dve.tensor_scalar(dst, src, s, None, ALU.mult).then_inc(tr_dve, 1)
                if m == XG - 1:
                    dve.wait_ge(ld_router, LDR)
                    dve.wait_ge(rw_zeroed, 1)
                    for k in range(KC):
                        dve.tensor_copy(rw_wide[:, k, 0:NE], rw_sb[:, k, :]).then_inc(rw_ready, 1)
                    dve.wait_ge(lg_done, 2)
                    dve.tensor_copy(lgT[1], lg_ps[1][:, :]).then_inc(lgT_ready, 1)
                if m == LG_AFTER - 1:
                    dve.wait_ge(logits_done, 1)
                    link(dve.tensor_copy(rbase[:, :], misc[:, NT * NE:(NT + 1) * NE]))
                    dve.tensor_tensor(logits[:, :, :], misc[:, 0:NT * NE].rearrange("p (n e) -> p n e", e=NE),
                                      over_tiles(rbase[:, :], slice(0, NT)), ALU.add).then_inc(logits_ready, 1)

            dve.wait_ge(ld_gru, LDG)
            link(dve.transpose(h0T[:, :, :].rearrange("p i q -> p (i q)"), h0_rows[:, :, :].rearrange("p i q -> p (i q)")))
            for i in range(NI):
                dve.tensor_copy(hist[:, TS - 1, i, :, 1], h0T[:, i, 0:B]).then_inc(hT_ready, 1)

            def score_tiles(tiles):
                dve.wait_ge(consts_ready, 1)
                dve.wait_ge(score_ready, 1)
                link(dve.tensor_tensor(sel[:, tiles, :], score[:, tiles, :], over_tiles(rbias[:, :], tiles), ALU.add))

            def find_best(tiles):
                link(dve.tensor_reduce(best[:, tiles], sel[:, tiles, :], AX.X, ALU.max))
                link(dve.tensor_tensor(hit[:, tiles, :], sel[:, tiles, :], over_experts(best[:, tiles]), ALU.is_equal))
                link(dve.tensor_tensor(hit[:, tiles, :], hit[:, tiles, :], over_tiles(rank[:, :], tiles), ALU.mult))

            def choose(k, tiles):
                link(dve.tensor_reduce(best[:, tiles], hit[:, tiles, :], AX.X, ALU.max))
                link(dve.tensor_tensor(first[:, tiles, :], hit[:, tiles, :], over_experts(best[:, tiles]), ALU.is_equal))
                if k == 0:
                    link(dve.tensor_copy(mask[:, tiles, :], first[:, tiles, :]))
                    link(dve.scalar_tensor_tensor(sel[:, tiles, :], first[:, tiles, :], -1e30, sel[:, tiles, :], ALU.mult, ALU.add))
                else:
                    link(dve.tensor_tensor(mask[:, tiles, :], mask[:, tiles, :], first[:, tiles, :], ALU.add))

            def sum_chosen(tiles):
                link(dve.tensor_tensor(score[:, tiles, :], score[:, tiles, :], mask[:, tiles, :], ALU.mult))
                link(dve.tensor_reduce(den[:, tiles], score[:, tiles, :], AX.X, ALU.add))
                link(dve.tensor_scalar(okay[:, tiles], den[:, tiles], 1e-9, None, ALU.is_gt))
                link(dve.tensor_scalar(rden[:, tiles], den[:, tiles], 1e-9, None, ALU.add))
                link(dve.reciprocal(rden[:, tiles], rden[:, tiles]))
                link(dve.scalar_tensor_tensor(rden[:, tiles], rden[:, tiles], SHARE, okay[:, tiles], ALU.mult, ALU.mult))
                link(dve.tensor_scalar(okay[:, tiles], okay[:, tiles], -SHARE / TOP_K, SHARE / TOP_K, ALU.mult, ALU.add))

            def make_gates(tiles):
                link(dve.tensor_tensor(score[:, tiles, :], score[:, tiles, :], over_experts(rden[:, tiles]), ALU.mult))
                link(dve.tensor_tensor(mask[:, tiles, :], mask[:, tiles, :], over_experts(okay[:, tiles]), ALU.mult))
                dve.tensor_tensor(gates_all[:, tiles, :], score[:, tiles, :], mask[:, tiles, :], ALU.add).then_inc(gates_ready, 1)

            early = slice(0, EARLY)
            score_tiles(early)
            for k in range(TOP_K):
                find_best(early)
                choose(k, early)
            sum_chosen(early)
            make_gates(early)

            def gate_biases():
                dve.wait_ge(ld_bias, LDB)
                dve.tensor_tensor(bias_x[:, :, :, :], bias_x[:, :, :, :], bias_h[:, :, :, :], ALU.add).then_inc(bias_ready, 1)

            late = slice(EARLY, NT)
            SETUP = {(-2, 15): gate_biases, (-1, 0): lambda: score_tiles(late),
                     (-1, 2): lambda: find_best(late), (-1, 4): lambda: choose(0, late),
                     (-1, 6): lambda: find_best(late), (-1, 8): lambda: choose(1, late),
                     (-1, 10): lambda: sum_chosen(late), (-1, 12): lambda: make_gates(late)}

            def shared_hidden(n, u, second, scan):
                ps = up_ps[UNITS.index(~u) % len(up_ps)]
                if not second:
                    dve.wait_ge(sig_done, NSH * (n + 2) + u + 1)
                    dve.scalar_tensor_tensor(sig[:, u, :], sig[:, u, :], 1.0, ps[:, 0:P], ALU.add, ALU.mult)\
                       .then_inc(silu_done, 1)
                else:
                    if not scan:
                        dve.wait_ge(silu_done, NSH * (n + 2) + u + 1)
                    dve.tensor_tensor(hid[:, u, :], sig[:, u, :], ps[:, P:2 * P], ALU.mult).then_inc(shared_ready, 1)

            def split_low(n, e):
                dve.wait_ge(gelu_ready, NE * (n + 2) + e + 1)
                dve.tensor_tensor(hid_low[:, e % HRING, :], hid_full[:, e % 2, :],
                                  hid_high[:, e % HRING, :].bitcast(F32), ALU.subtract).then_inc(low_ready, 1)

            def accumulate(n, g, scan):
                e, ps = GROUPS[g], dn_bank(g)
                dve.wait_ge(dn_done, NDN * (n + 2) + g + 1)
                if g == 0:
                    dve.wait_ge(xg_loaded, 32 * (n + 3))
                if not scan and (g > 0 or above(n, -1)):
                    dve.wait_ge(acc_done, NDN * (n + 2) + g)
                if g == NDN - 1 and above(n, -1):
                    dve.wait_ge(x1T_done, n + 2)
                    dve.wait_ge(x1_stored, 16 * (n + 2))
                dve.scalar_tensor_tensor((x1_cur if g == NDN - 1 else acc)[:, :], ps[:, 0:C],
                                         0.5 * SHARE if e == SHARED else gates_cur[:, e:e + 1],
                                         (x_cur if g == 0 else acc)[:, :], ALU.mult, ALU.add).then_inc(acc_done, 1)

            def add_bias(n, q):
                dve.wait_ge(xp_done, GATES * (n + 1) + q + 1)
                if isinstance(n, int) and n == -1:
                    dve.wait_ge(bias_ready, 1)
                else:
                    dve.wait_ge(xp_stored, 16 * (n + 1))
                    dve.wait_ge(xs_second, 16 * NG * (n + 1))
                    if q == GATES - 1:
                        dve.wait_ge(seeded_zc, TS * n + HALF)
                cols = slice(q * C, (q + 1) * C)
                dve.tensor_tensor(xproj[:, :, :].rearrange("p j c -> p (j c)")[:, cols],
                                  misc[:, 0:C],
                                  bias_x[:, :, :, :].rearrange("p j g c -> p (j g c)")[:, cols],
                                  ALU.add).then_inc(xp_ready, 1)

            def finish_out(n):
                dve.wait_ge(y_done, n)
                if above(n, 2):
                    dve.wait_ge(y_ready, n - 1)
                dve.tensor_tensor(y_bias[:, :], misc[:, 0:C], bias_q[:, :], ALU.add).then_inc(y_bias_done, 1)

            def add_x1(n):
                dve.wait_ge(y_bias_done, n)
                dve.wait_ge(x_res_loaded, 16 * n)
                if above(n, 2):
                    dve.wait_ge(out_stored, 16 * (n - 1))
                dve.tensor_tensor(y_out[:, :], y_bias[:, :], x_res[:, :], ALU.add).then_inc(y_ready, 1)

            def body(n, scan, moe, proj, outs, more):
                for s in range(TS):
                    old = hist[:, (s - 1) % TS, :, :, 1]
                    g = NI * (TS * n + s)
                    if scan:
                        for i in range(NI):
                            dve.wait_ge(tr_ready, g + i + 1)
                            dve.transpose(t_rT[:, i, :], t_r[:, i, :]).then_inc(trT_done, 1)
                        for i in range(NI):
                            dve.wait_ge(trT_done, g + i + 1)
                            dve.scalar_tensor_tensor(rhT[:, i, :], t_rT[:, i, 0:B], 1.0, old[:, i, :], ALU.add, ALU.mult)\
                               .then_inc(rhT_ready, 1)
                        dve.wait_ge(tz_ready, TS * n + s + 1)
                        dve.transpose(t_zT[:, :, :].rearrange("p i q -> p (i q)"), t_z[:, :, :].rearrange("p i q -> p (i q)"))\
                           .then_inc(tzT_done, 1)
                    if s == 0 and proj:
                        accumulate(n - 1, NDN - 2, scan)
                    if moe:
                        for u, second in SILU_GAP1.get(s, []):
                            shared_hidden(n, u, second, scan)
                    if moe and s in LOW_GAP1:
                        split_low(n, LOW_GAP1[s])
                    if scan:
                        dve.wait_ge(tzT_done, TS * n + s + 1)
                        dve.tensor_scalar(factors[:, :, :, 1], t_zT[:, :, 0:B], -0.5, 0.5, ALU.mult, ALU.add).then_inc(a_ready, 1)
                        dve.wait_ge(a_ready, TS * n + s + 1)
                        dve.scalar_tensor_tensor(terms[:, :, 0:B, 1], factors[:, :, :, 1], 1.0, old, ALU.subtract, ALU.mult)
                        for i in range(NI):
                            dve.wait_ge(th_ready, g + i + 1)
                            dve.transpose(terms[:, i, :, 0], t_h[:, i, :]).then_inc(thT_done, 1)
                        for i in range(NI):
                            dve.wait_ge(thT_done, g + i + 1)
                            dve.tensor_tensor_scan(hist[:, s, i, :, :].rearrange("p b e -> p (b e)"),
                                                   factors[:, i, :, :].rearrange("p b e -> p (b e)"),
                                                   terms[:, i, 0:B, :].rearrange("p b e -> p (b e)"),
                                                   0.0, ALU.mult, ALU.subtract).then_inc(hT_ready, 1)
                    if s == 0 and proj:
                        accumulate(n - 1, NDN - 1, scan)
                    if proj and s >= XP_STEP and (s - XP_STEP) % 2 == 1 and s < Y_STEP:
                        add_bias(n, (s - XP_STEP) // 2)
                    if moe:
                        for u, second in SILU_GAP2.get(s, []):
                            shared_hidden(n, u, second, scan)
                    if outs and s == Y_STEP + NI - 1:
                        finish_out(n)
                    if outs and s == OUT_STEP:
                        add_x1(n)
                    if moe and s in LOW_GAP2:
                        split_low(n, LOW_GAP2[s])
                    if moe and s in ADD_GAP2:
                        accumulate(n, ADD_GAP2[s], scan)
                    if isinstance(n, int) and (n, s) in SETUP:
                        SETUP[n, s]()
                    if isinstance(n, int) and n == -2:
                        e = s - SPLIT_STEP
                        if 0 <= e < NE:
                            dve.wait_ge(we2_high_ready, e + 1)
                            dve.tensor_tensor(we2_low[:, e, :, :], we2_raw[:, e, :, :], we2_high[:, e, :, :].bitcast(F32), ALU.subtract)\
                               .then_inc(we2_split, 1)

            iterations(dve, body)

        @block.tensor
        def _(pe):
            pe.wait_ge(ident_ready, 1)
            pe.wait_ge(consts_ready, 1)

            def transposes(m):
                if m >= 4:
                    pe.wait_ge(tr_act if m % 2 == 0 else tr_dve, (m - 4) // 2 + 1)
                dst = tr_ps[m % 4]
                if m < XG:
                    blocks = [x_all[:, (4 * m + i) // KC, ((4 * m + i) % KC) * P:((4 * m + i) % KC + 1) * P] for i in range(4)]
                elif m == XG:
                    blocks = [cond_tok[:, k * P:(k + 1) * P] for k in range(KC)]
                else:
                    r, kind, gate, k = WGROUPS[m - XG - 1]
                    blocks = [(raw[r] if kind == "x" else ordered[r])[:, o, k * P:(k + 1) * P] for o in range(KC)]
                for i, blk in enumerate(blocks):
                    last = pe.transpose(dst[:, i * P:(i + 1) * P], blk, ident[:, :])
                last.then_inc(tr_done, 1)

            for h in range(2):
                pe.wait_ge(ld_x[h], LDX)
                for m in range(h * XG // 2, (h + 1) * XG // 2):
                    transposes(m)
            pe.wait_ge(ld_router, LDR)
            transposes(XG)
            pe.wait_ge(rw_ready, KC)
            pe.wait_ge(tr_act, XG // 2 + 1)
            pe.wait_ge(tr_dve, XG // 2)
            for h in range(2):
                for k in range(KC):
                    for j in range(NG):
                        first_tile = (h * NG + j) * TG
                        last = pe.matmul(lg_ps[h][Q * j:Q * (j + 1), :], rw_wide[:, k, :],
                                         xT_all[:, first_tile:first_tile + TG, k, :],
                                         start=(k == 0), stop=(k == KC - 1), tile_position=(0, Q * j), skip_group_check=True)
                last.then_inc(lg_done, 1)
            pe.wait_ge(ld_gru, LDG)
            for m in range(XG + 1, LG_AFTER + 1):
                transposes(m)
            for k in range(KC):
                pe.matmul(misc[:, NT * NE:(NT + 1) * NE], condT[:, k, :], rw_sb[:, KC + k, :], start=(k == 0), stop=(k == KC - 1))
            pe.wait_ge(lgT_ready, 2)
            for h in range(2):
                for i in range(TG):
                    last = pe.matmul(misc[:, 0:NT * NE].rearrange("p (h j i e) -> p h i j e", h=2, j=NG, i=TG)[:, h, i, :, :],
                                     lgT[h][:, i * P:(i + 1) * P],
                                     ident[:, :].rearrange("p (j q) -> p j q", j=NG)[:, :, 0:NE], start=True, stop=True)
            last.then_inc(logits_done, 1)
            pe.wait_ge(ordered_done, len(ordered) * KC)
            for m in range(LG_AFTER + 1, NTR):
                transposes(m)
            pe.wait_ge(tr_act, (NTR + 1) // 2)
            pe.wait_ge(tr_dve, NTR // 2)
            for p in (r_ps, zc_ps):
                pe.matmul(p[:, 0:2 * GW], zeros[:, :], zeros[:, 0:2 * GW], start=True, stop=True).then_inc(bits_set, 1)

            def up(n, m):
                place, half, k = m // UP_MM, m % UP_MM // KC, m % KC
                u, ring = UNITS[place], len(up_ps)
                if m % UP_MM == 0:
                    if place == 0:
                        pe.wait_ge(xT_loaded, 16 * (n + 3))
                        if isinstance(n, int) and n == -2:
                            pe.wait_ge(ld_w13, 32)
                            pe.wait_ge(ld_we1, 16)
                    if place >= ring:
                        before = UNITS[place - ring]
                        if before < 0:
                            pe.wait_ge(shared_ready, NSH * (n + 2) + ~before + 1)
                        else:
                            pe.wait_ge(gelu_ready, NE * (n + 2) + before + 1)
                    elif above(n, -1):
                        pe.wait_ge(gelu_ready, NE * (n + 1) + UNITS[place - ring] + 1)
                if u < 0:
                    w = (w1_sb, w3_sb)[half][:, k, ~u * P:(~u + 1) * P]
                else:
                    w = we1_sb[:, u, k, half * P:(half + 1) * P]
                last = pe.matmul(up_ps[place % ring][:, half * P:(half + 1) * P], w, xT_cur[:, k, :],
                                 start=(k == 0), stop=(k == KC - 1))
                if m % UP_MM == UP_MM - 1:
                    last.then_inc(up_done, 1)

            def down(n, m):
                g, k, part = DN_MM[m]
                e, ps = GROUPS[g], dn_bank(g)
                first = m == 0 or DN_MM[m - 1][0] != g
                last = m + 1 == len(DN_MM) or DN_MM[m + 1][0] != g
                if first:
                    if g == 0 and above(n, -1):
                        pe.wait_ge(acc_done, NDN * (n + 2))
                    if 2 <= g < NDN - 1:
                        pe.wait_ge(acc_done, NDN * (n + 2) + g - 1)
                if e == SHARED:
                    pe.wait_ge(shared_ready, NSH * (n + 2) + k + 1)
                    if k == 0 and isinstance(n, int) and n == -2:
                        pe.wait_ge(ld_w2, 16)
                    lhsT, rhs = hid[:, k, :], w2_sb[:, k, :]
                else:
                    if first:
                        pe.wait_ge(gelu_ready, NE * (n + 2) + e + 1)
                        if isinstance(n, int) and n == -2:
                            pe.wait_ge(we2_split, e + 1)
                    if (k, part) == (0, "low high"):
                        pe.wait_ge(low_ready, NE * (n + 2) + e + 1)
                    h = hid_low if part == "low high" else hid_high
                    w = we2_low if part == "high low" else we2_high
                    lhsT, rhs = h[:, e % HRING, k * P:(k + 1) * P], w[:, e, k, :]
                ins = pe.matmul(ps[:, 0:C], lhsT, rhs, start=first, stop=last)
                if last:
                    ins.then_inc(dn_done, 1)

            def free_misc(n, proj, outs):
                if outs:
                    pe.wait_ge(y_bias_done, n)
                elif proj:
                    pe.wait_ge(xp_ready, GATES * (n + 2))
                else:
                    pe.wait_ge(logits_ready, 1)

            def transpose_x1(n):
                pe.wait_ge(acc_done, NDN * (n + 2))
                for k in range(KC):
                    last = pe.transpose(misc[:, k * P:(k + 1) * P], x1_cur[:, k * P:(k + 1) * P], ident[:, :])
                last.then_inc(x1T_done, 1)

            def project(n, q, k):
                if k == 0:
                    if q == 0:
                        pe.wait_ge(x1T_ready, n + 2)
                    if q > 0 or above(n, 0):
                        pe.wait_ge(xp_ready, GATES * (n + 1) + q)
                last = pe.matmul(misc[:, 0:C], x1T[:, k, :],
                                 wxT[:, k, :, :, :].rearrange("p j g c -> p (j g c)")[:, q * C:(q + 1) * C],
                                 start=(k == 0), stop=(k == KC - 1))
                if k == KC - 1:
                    last.then_inc(xp_done, 1)

            def output(n, i, proj):
                if i == 0:
                    pe.wait_ge(yst_ready, n)
                    if proj:
                        pe.wait_ge(xp_ready, GATES * (n + 2))
                    else:
                        pe.wait_ge(y_bias_done, n - 1)
                last = pe.matmul(misc[:, 0:C], yst[:, i, :], wqT[:, i, :], start=(i == 0), stop=(i == NI - 1))
                if i == NI - 1:
                    last.then_inc(y_done, 1)

            def gate_product(ps, col, gate, lhsT, i):
                for j in reversed(range(NG)):
                    last = pe.matmul(ps[Q * j:Q * j + B, col:col + GW], lhsT[:, i, :],
                                     whT[:, gate, i, j * GW:(j + 1) * GW], start=False, stop=(i == NI - 1),
                                     tile_position=(0, Q * j), skip_group_check=True)
                return last

            def keep_busy(count):
                for _ in range(count):
                    pe.matmul(up_ps[0][:, 0:2 * P], zeros[:, :], w1_sb[:, 0, 0:2 * P], start=True, stop=True).then_inc(kept_busy, 1)

            def body(n, scan, moe, proj, outs, more):
                for s in range(TS):
                    hT = hist[:, (s - 1) % TS, :, :, 1]
                    g = NI * (TS * n + s)
                    if scan:
                        for i in range(NI):
                            pe.wait_ge(hT_ready, g + i + 1)
                            if isinstance(n, int) and n == 0 and s == 0 and i == 0:
                                pe.wait_ge(seeded_r, 1)
                            last = gate_product(r_ps, 0, 0, hT, i)
                        last.then_inc(r_done, 1)
                        pe.wait_ge(seeded_zc, TS * n + s + 1)
                        for i in range(NI):
                            last = gate_product(zc_ps, 0, 1, hT, i)
                        last.then_inc(z_done, 1)
                    if proj and s == XP_STEP - 1:
                        transpose_x1(n)
                    if proj and XP_STEP <= s < Y_STEP:
                        project(n, (s - XP_STEP) // 2, (s - XP_STEP) % 2)
                    if outs and Y_STEP <= s < Y_STEP + NI:
                        output(n, s - Y_STEP, proj)
                    if proj and s == 0:
                        for m in DN_REST:
                            down(n - 1, m)
                    if moe:
                        for m in UP_GAP1[s]:
                            up(n, m)
                        for m in DN_GAP1[s]:
                            down(n, m)
                    elif scan and not (proj and XP_STEP - 1 <= s < Y_STEP or Y_STEP <= s < Y_STEP + NI):
                        keep_busy(1)
                    if scan:
                        for i in range(NI):
                            pe.wait_ge(rhT_ready, g + i + 1)
                            if i == 0:
                                pe.wait_ge(tz_ready, TS * n + s + 1)
                            last = gate_product(zc_ps, GW, 2, rhT, i)
                        last.then_inc(c_done, 1)
                    if moe:
                        for m in UP_GAP2[s]:
                            up(n, m)
                        for m in DN_GAP2[s]:
                            if DN_MM[m] == (NDN - 1, *PARTS[0]):
                                free_misc(n, proj, outs)
                            down(n, m)
                    elif scan:
                        keep_busy(2)

            iterations(pe, body)


_INS = ['x', 'cond_1024', 'L0_cond_router_W', 'L0_cond_router_bias', 'L0_cond_w1', 'L0_cond_w3', 'L0_cond_w2',
        'L0_cond_W1e', 'L0_cond_W2e', 'L1_cond_Wxz', 'L1_cond_bxz', 'L1_cond_Whz', 'L1_cond_bhz', 'L1_cond_Wxr',
        'L1_cond_bxr', 'L1_cond_Whr', 'L1_cond_bhr', 'L1_cond_Wxh', 'L1_cond_bxh', 'L1_cond_Whh', 'L1_cond_bhh',
        'L1_cond_Whq', 'L1_cond_bhq']


def kernel(**inputs):
    import numpy as np
    import concourse.bacc as bacc
    from concourse.bass_utils import run_bass_kernel_spmd

    nc = bacc.Bacc("TRN2", target_bir_lowering=False, num_devices=1)
    arrays, args = {}, []
    for name in _INS:
        a = np.ascontiguousarray(inputs[name])
        arrays[f"in_{name}"] = a
        args.append(nc.dram_tensor(f"in_{name}", a.shape, mybir.dt.from_np(a.dtype), kind="ExternalInput").ap())
    args.append(nc.dram_tensor("out_0", arrays["in_x"].shape, mybir.dt.float32, kind="ExternalOutput").ap())
    moe_then_gru(nc, *args)
    r = run_bass_kernel_spmd(nc, [arrays], core_ids=[0])
    return r.results[0]["out_0"]
```
